# Optimizing a Trainium2 kernel written in Bass

```python
import numpy as np
import jax
import jax.numpy as jnp

def _softmax(x, axis=-1):
    return jax.nn.softmax(x, axis=axis)

def _gelu(x):
    return jax.nn.gelu(x, approximate=True)

def _silu(x):
    return jax.nn.silu(x)

def _sigmoid(x):
    return jax.nn.sigmoid(x)

def _layernorm(x, axis=-1, eps=1e-05):
    m = jnp.mean(x, axis=axis, keepdims=True)
    v = jnp.var(x, axis=axis, keepdims=True)
    return (x - m) / jnp.sqrt(v + eps)

def _scatter_add(tgt, idx, src, axis=0):
    return tgt.at[idx].add(src)

def _segment_sum(src, seg, n):
    return jax.ops.segment_sum(src, seg, n)
kernel_name = 'mk_seq_postln_d1_jaxref_r8_4c72c0'

def setup_inputs(seed: int=0):
    np.random.seed(seed)
    _w = jnp.asarray

    def _L0_attn_setup():
        import jax, jax.numpy as jnp
        import numpy as np
        LN_EPS = 1e-05
        NEG_INF = -1e+38

        def _layer_norm(x, g, b):
            mu = x.mean(-1, keepdims=True)
            var = ((x - mu) ** 2).mean(-1, keepdims=True)
            return (x - mu) * jax.lax.rsqrt(var + LN_EPS) * g + b

        def _wkv(w, u, k, v):
            B, T, C = k.shape
            kt = jnp.swapaxes(k, 0, 1)
            vt = jnp.swapaxes(v, 0, 1)
            aa0 = jnp.zeros((B, C), k.dtype)
            bb0 = jnp.zeros((B, C), k.dtype)
            pp0 = jnp.full((B, C), NEG_INF, k.dtype)

            def step(carry, inp):
                aa, bb, pp = carry
                kk, vv = inp
                p = jnp.maximum(pp, u + kk)
                e1 = jnp.exp(pp - p)
                e2 = jnp.exp(u + kk - p)
                y = (e1 * aa + e2 * vv) / (e1 + e2)
                p2 = jnp.maximum(pp + w, w + kk)
                e1u = jnp.exp(pp + w - p2)
                e2u = jnp.exp(w + kk - p2)
                aa2 = e1u * aa + e2u * vv
                bb2 = e1u + e2u
                pp2 = p2 + jnp.log(bb2)
                return ((aa2, bb2, pp2), y)
            _, ys = jax.lax.scan(step, (aa0, bb0, pp0), (kt, vt))
            return jnp.swapaxes(ys, 0, 1)

        def _shift(h):
            return jnp.pad(h[:, :-1, :], ((0, 0), (1, 0), (0, 0)))
        key = jax.random.key(seed)
        B, T, C = (8, 256, 128)
        ks = jax.random.split(key, 12)
        s = 0.02
        return {'x': jax.random.normal(ks[0], (B, T, C), jnp.float32), 'time_decay': jax.random.normal(ks[1], (C,), jnp.float32) * 0.01, 'time_first': jax.random.normal(ks[2], (C,), jnp.float32) * 0.01, 'w_tk': jax.random.normal(ks[3], (C, C), jnp.float32) * s, 'w_tv': jax.random.normal(ks[4], (C, C), jnp.float32) * s, 'w_tr': jax.random.normal(ks[5], (C, C), jnp.float32) * s, 'w_ck': jax.random.normal(ks[6], (C, 4 * C), jnp.float32) * s, 'w_cv': jax.random.normal(ks[7], (4 * C, C), jnp.float32) * s, 'w_cr': jax.random.normal(ks[8], (C, C), jnp.float32) * s, 'ln1_g': jnp.ones((C,), jnp.float32), 'ln1_b': jnp.zeros((C,), jnp.float32), 'ln2_g': jnp.ones((C,), jnp.float32), 'ln2_b': jnp.zeros((C,), jnp.float32), 'mix_k': jnp.ones((1, 1, C), jnp.float32), 'mix_v': jnp.ones((1, 1, C), jnp.float32), 'mix_r': jnp.ones((1, 1, C), jnp.float32), 'cmix_k': jnp.ones((1, 1, C), jnp.float32), 'cmix_r': jnp.ones((1, 1, C), jnp.float32)}
    _L0_attn_in = _L0_attn_setup()

    def _L0_ffn_setup():
        import jax, jax.numpy as jnp
        import numpy as np
        key = jax.random.key(seed)
        ks = jax.random.split(key, 4)
        B, T, M, E, F = (4, 256, 128, 8, 512)
        hidden_states = jax.random.normal(ks[0], (B, T, M), dtype=jnp.float32)
        wg = jax.random.normal(ks[1], (M, E), dtype=jnp.float32) * (1.0 / np.sqrt(M))
        w1 = jax.random.normal(ks[2], (E, M, F), dtype=jnp.float32) * (1.0 / np.sqrt(M))
        b1 = jnp.zeros((E, F), dtype=jnp.float32)
        w2 = jax.random.normal(ks[3], (E, F, M), dtype=jnp.float32) * (1.0 / np.sqrt(F))
        b2 = jnp.zeros((E, M), dtype=jnp.float32)
        return {'hidden_states': hidden_states, 'wg': wg, 'w1': w1, 'b1': b1, 'w2': w2, 'b2': b2}
    _L0_ffn_in = _L0_ffn_setup()
    _d = {'L0_attn_x': _L0_attn_in['x'], 'L0_attn_time_decay': _L0_attn_in['time_decay'], 'L0_attn_time_first': _L0_attn_in['time_first'], 'L0_attn_w_tk': _L0_attn_in['w_tk'], 'L0_attn_w_tv': _L0_attn_in['w_tv'], 'L0_attn_w_tr': _L0_attn_in['w_tr'], 'L0_attn_w_ck': _L0_attn_in['w_ck'], 'L0_attn_w_cv': _L0_attn_in['w_cv'], 'L0_attn_w_cr': _L0_attn_in['w_cr'], 'L0_attn_ln1_g': _L0_attn_in['ln1_g'], 'L0_attn_ln1_b': _L0_attn_in['ln1_b'], 'L0_attn_ln2_g': _L0_attn_in['ln2_g'], 'L0_attn_ln2_b': _L0_attn_in['ln2_b'], 'L0_attn_mix_k': _L0_attn_in['mix_k'], 'L0_attn_mix_v': _L0_attn_in['mix_v'], 'L0_attn_mix_r': _L0_attn_in['mix_r'], 'L0_attn_cmix_k': _L0_attn_in['cmix_k'], 'L0_attn_cmix_r': _L0_attn_in['cmix_r'], 'L0_ffn_wg': _L0_ffn_in['wg'], 'L0_ffn_w1': _L0_ffn_in['w1'], 'L0_ffn_b1': _L0_ffn_in['b1'], 'L0_ffn_w2': _L0_ffn_in['w2'], 'L0_ffn_b2': _L0_ffn_in['b2']}
    _x0 = _d['L0_attn_x']
    _d['L0_attn_x'] = jax.random.normal(jax.random.fold_in(jax.random.key(seed), 1), (2, 2048, 128), dtype=_x0.dtype)
    del _x0
    return _d

def reference(L0_attn_x, L0_attn_time_decay, L0_attn_time_first, L0_attn_w_tk, L0_attn_w_tv, L0_attn_w_tr, L0_attn_w_ck, L0_attn_w_cv, L0_attn_w_cr, L0_attn_ln1_g, L0_attn_ln1_b, L0_attn_ln2_g, L0_attn_ln2_b, L0_attn_mix_k, L0_attn_mix_v, L0_attn_mix_r, L0_attn_cmix_k, L0_attn_cmix_r, L0_ffn_wg, L0_ffn_w1, L0_ffn_b1, L0_ffn_w2, L0_ffn_b2):

    def _L0_attn_ref(x, time_decay, time_first, w_tk, w_tv, w_tr, w_ck, w_cv, w_cr, ln1_g, ln1_b, ln2_g, ln2_b, mix_k, mix_v, mix_r, cmix_k, cmix_r):
        import jax, jax.numpy as jnp
        import numpy as np
        LN_EPS = 1e-05
        NEG_INF = -1e+38

        def _layer_norm(x, g, b):
            mu = x.mean(-1, keepdims=True)
            var = ((x - mu) ** 2).mean(-1, keepdims=True)
            return (x - mu) * jax.lax.rsqrt(var + LN_EPS) * g + b

        def _wkv(w, u, k, v):
            B, T, C = k.shape
            kt = jnp.swapaxes(k, 0, 1)
            vt = jnp.swapaxes(v, 0, 1)
            aa0 = jnp.zeros((B, C), k.dtype)
            bb0 = jnp.zeros((B, C), k.dtype)
            pp0 = jnp.full((B, C), NEG_INF, k.dtype)

            def step(carry, inp):
                aa, bb, pp = carry
                kk, vv = inp
                p = jnp.maximum(pp, u + kk)
                e1 = jnp.exp(pp - p)
                e2 = jnp.exp(u + kk - p)
                y = (e1 * aa + e2 * vv) / (e1 + e2)
                p2 = jnp.maximum(pp + w, w + kk)
                e1u = jnp.exp(pp + w - p2)
                e2u = jnp.exp(w + kk - p2)
                aa2 = e1u * aa + e2u * vv
                bb2 = e1u + e2u
                pp2 = p2 + jnp.log(bb2)
                return ((aa2, bb2, pp2), y)
            _, ys = jax.lax.scan(step, (aa0, bb0, pp0), (kt, vt))
            return jnp.swapaxes(ys, 0, 1)

        def _shift(h):
            return jnp.pad(h[:, :-1, :], ((0, 0), (1, 0), (0, 0)))
        h = _layer_norm(x, ln1_g, ln1_b)
        hp = _shift(h)
        xk = h * mix_k + hp * (1.0 - mix_k)
        xv = h * mix_v + hp * (1.0 - mix_v)
        xr = h * mix_r + hp * (1.0 - mix_r)
        k = xk @ w_tk
        v = xv @ w_tv
        r = jax.nn.sigmoid(xr @ w_tr)
        y = _wkv(time_decay, time_first, k, v)
        x = x + r * y
        h2 = _layer_norm(x, ln2_g, ln2_b)
        hp2 = _shift(h2)
        ck = h2 * cmix_k + hp2 * (1.0 - cmix_k)
        cr = h2 * cmix_r + hp2 * (1.0 - cmix_r)
        kk = jnp.square(jax.nn.relu(ck @ w_ck))
        x = x + jax.nn.sigmoid(cr @ w_cr) * (kk @ w_cv)
        return x

    def _L0_ffn_ref(hidden_states, wg, w1, b1, w2, b2):
        import jax, jax.numpy as jnp
        import numpy as np
        B, T, M = hidden_states.shape
        E = wg.shape[1]
        S = B * T
        MIN_CAPACITY = 4
        C = max((S + E - 1) // E, MIN_CAPACITY)
        x = hidden_states.reshape(S, M)
        logits = x @ wg
        gates = jax.nn.softmax(logits, axis=-1)
        idx = jnp.argmax(gates, axis=-1)
        mask1 = jax.nn.one_hot(idx, E, dtype=gates.dtype)
        l_aux = jnp.sum(gates.mean(0) * mask1.mean(0)) * E
        locations1 = jnp.cumsum(mask1, axis=0) - 1.0
        mask1 = mask1 * (locations1 < C)
        gates1_s = jnp.sum(gates * mask1, axis=1)
        loc_s = jnp.sum(locations1 * mask1, axis=1).astype(jnp.int32)
        loc_sc = jax.nn.one_hot(loc_s, C, dtype=gates.dtype)
        combine_weights = jnp.einsum('se,sc->sec', gates1_s[:, None] * mask1, loc_sc)
        dispatch_mask = (combine_weights > 0).astype(x.dtype)
        dispatched = jnp.einsum('sec,sm->ecm', dispatch_mask, x)
        h = jax.nn.gelu(jnp.einsum('ecm,emf->ecf', dispatched, w1) + b1[:, None, :])
        expert_out = jnp.einsum('ecf,efm->ecm', h, w2) + b2[:, None, :]
        out = jnp.einsum('sec,ecm->sm', combine_weights, expert_out)
        return out.reshape(B, T, M)
    x = L0_attn_x
    x = _layernorm(x + _L0_attn_ref(x, L0_attn_time_decay, L0_attn_time_first, L0_attn_w_tk, L0_attn_w_tv, L0_attn_w_tr, L0_attn_w_ck, L0_attn_w_cv, L0_attn_w_cr, L0_attn_ln1_g, L0_attn_ln1_b, L0_attn_ln2_g, L0_attn_ln2_b, L0_attn_mix_k, L0_attn_mix_v, L0_attn_mix_r, L0_attn_cmix_k, L0_attn_cmix_r), axis=-1)
    x = _layernorm(x + _L0_ffn_ref(x, L0_ffn_wg, L0_ffn_w1, L0_ffn_b1, L0_ffn_w2, L0_ffn_b2), axis=-1)
    return x

_drawn_inputs = setup_inputs


def setup_inputs(seed=0):
    import zlib

    import numpy as np

    out = dict(_drawn_inputs(seed))
    spreads = {'L0_attn_ln1_g': (1.0, 0.2),
     'L0_attn_ln1_b': (0.0, 0.1),
     'L0_attn_ln2_g': (1.0, 0.6),
     'L0_attn_ln2_b': (0.0, 0.586),
     'L0_attn_mix_k': (1.0, 0.6),
     'L0_attn_mix_v': (1.0, 0.588),
     'L0_attn_mix_r': (1.0, 0.6),
     'L0_attn_cmix_k': (1.0, 0.6),
     'L0_attn_cmix_r': (1.0, 0.6),
     'L0_ffn_b1': (0.0, 0.334),
     'L0_ffn_b2': (0.0, 0.1)}
    factors = {'L0_attn_time_first': 200.0, 'L0_attn_w_ck': 2.828, 'L0_attn_w_cr': 6.385}
    for name, (base, spread) in spreads.items():
        noise = np.random.default_rng([zlib.crc32(name.encode()), seed]).standard_normal(out[name].shape)
        drawn = base * np.exp(spread * noise) if base else spread * noise
        out[name] = jnp.asarray(drawn.astype(out[name].dtype))
    for name, factor in factors.items():
        out[name] = (out[name] * factor).astype(out[name].dtype)
    return out
```

```python
from contextlib import ExitStack

import concourse.bass as bass
from concourse import mybir

ALU = mybir.AluOpType
ACT = mybir.ActivationFunctionType
AX = mybir.AxisListType
F32 = mybir.dt.float32
BF16 = mybir.dt.bfloat16
U32 = mybir.dt.uint32

P = 128
LN_EPS = 1e-05
NEG_INF = -1e38
BIG = 3e38
W_, U_, G1, B1, G2, B2, MK, MV, MR, CK, CR = range(11)
NVEC = 11


def rwkv_moe_kernel(nc, x, time_decay, time_first, w_tk, w_tv, w_tr, w_ck, w_cv, w_cr,
                    ln1_g, ln1_b, ln2_g, ln2_b, mix_k, mix_v, mix_r, cmix_k, cmix_r,
                    wg, w1, b1, w2, b2, out):
    B, T, C = x.shape
    E, _, F = w1.shape
    N = B * T
    TILE = P
    CH = 512
    TPC = CH // TILE
    NCH = N // CH
    CPB = T // CH
    FB = F // P
    CAP = (N + E - 1) // E
    SPE = CAP // TILE
    ROW = C + 2
    GATE, TOK = C, C + 1
    TRASH = E * CAP
    assert C == P and CAP == CH and F == 4 * P

    xf = x.rearrange("b (k j p) c -> (b k) p j c", p=TILE, j=TPC)
    of = out.rearrange("b (k j p) c -> (b k) p j c", p=TILE, j=TPC)
    out_rows = out.rearrange("b t c -> (b t) c")
    disp = nc.dram_tensor("disp", [TRASH + N, ROW], F32, kind="Internal").ap()
    disp_t = disp[0:TRASH, :].rearrange("(e j p) r -> e p j r", p=TILE, j=SPE)

    with ExitStack() as ctx:
        def sb(name, shape, dt=F32):
            return ctx.enter_context(nc.sbuf_tensor(name, shape, dt))

        def sem(name):
            return ctx.enter_context(nc.semaphore(name))

        def bank(name):
            return ctx.enter_context(nc.psum_tensor(name, [P, 512], F32))

        ps_k, ps_vr, ps_ta, ps_tb = bank("ps_k"), bank("ps_vr"), bank("ps_ta"), bank("ps_tb")
        ps_h = [bank("ps_h0"), bank("ps_h1")]
        ps_cv, ps_cr = bank("ps_cv"), bank("ps_cr")

        x_sb = sb("x_sb", [P, NCH, TPC, C])
        vrows = sb("vrows", [NVEC + E * FB, P])
        vcol = sb("vcol", [P, NVEC + E * FB])
        wt_sb = sb("wt_sb", [P, 4, C])
        wm_sb = sb("wm_sb", [P, 4, 2, C])
        wck_sb = sb("wck_sb", [P, F])
        wcv_sb = sb("wcv_sb", [P, FB, C])
        wg_sb = sb("wg_sb", [P, E])
        w1_sb = sb("w1_sb", [P, E, F])
        w2_sb = sb("w2_sb", [P, E, FB, C])
        b2_sb = sb("b2_sb", [P, E, C])
        ident = sb("ident", [P, P])
        tri = sb("tri", [P, P], BF16)
        ones = sb("ones", [P, P], BF16)
        mhalf = sb("mhalf", [P, TPC])
        iota_e = sb("iota_e", [P, TPC, E])
        iota_e8 = sb("iota_e8", [P, TPC, E])
        tokf = sb("tokf", [P, NCH, TPC])
        omix = sb("omix", [P, 5])
        nuh = sb("nuh", [P, 1])
        fill = sb("fill", [P, SPE, ROW])
        hT = sb("hT", [P, B, T + 1])
        h2T = sb("h2T", [P, B, T + 1])
        def two(name, shape, dt=F32):
            return [sb(f"{name}{i}", shape, dt) for i in range(2)]

        mv1, mv2, mv3 = two("mv1", [P, TPC, 2]), two("mv2", [P, TPC, 2]), two("mv3", [P, TPC, 2])
        st = two("st", [P, TPC, 6])
        lnw = sb("lnw", [P, 3, 2, 4, TPC])
        xn = two("xn", [P, TPC, C])
        Mx = two("Mx", [P, CH + 1])
        Sx = two("Sx", [P, CH + 1])
        Ax = two("Ax", [P, CH + 1])
        G = two("G", [P, CH])
        EF = two("EF", [P, 2, CH])
        LS = two("LS", [P, CH])
        AB = two("AB", [P, 2, CH])
        V = two("V", [P, CH])
        TH = two("TH", [P, CH])
        THR = two("THR", [P, CH])
        Y = two("Y", [P, CH])
        x1 = two("x1", [P, TPC, C])
        x2n = two("x2n", [P, TPC, C])
        cx = two("cx", [P, CH])
        rl = two("rl", [P, CH])
        kk = two("kk", [P, FB, CH])
        thc = two("thc", [P, TPC, C])
        z = two("z", [P, TPC, C])
        rows = two("rows", [P, TPC, ROW])
        drp = two("drp", [P, TPC, C])
        dsc = sb("dsc", [P, 3, TPC])
        x3T = sb("x3T", [P, CH])
        mx = sb("mx", [P, TPC])
        lg = sb("lg", [P, TPC, E])
        ex = sb("ex", [P, TPC, E])
        sm = sb("sm", [P, TPC])
        cand = sb("cand", [P, TPC, E])
        eidx = sb("eidx", [P, TPC])
        oh = sb("oh", [P, TPC, E], BF16)
        ohs = sb("ohs", [P, 2, E], BF16)
        ohr = sb("ohr", [P, E])
        loc8 = sb("loc8", [P, TPC, E])
        loc = sb("loc", [P, TPC])
        keep = sb("keep", [P, TPC])
        slot = sb("slot", [P, TPC])
        sidx = two("sidx", [P, TPC], U32)
        er, eT = rows, V
        tid = two("tid", [P, SPE], U32)

        S = {}

        def s(name):
            if name not in S:
                S[name] = sem(name)
            return S[name]

        names = """w_in we_in v_in vt vcol cst id0 fillset disp_fill out_drop wmix mset hzero
            ln1_st ln1_mv ln_pool xn xnT hT kmm vmm rmm m0 mscan gdone efin efexp s0 sscan lns
            delta abin abexp th v_sb thr bv a0 ascan df q y ry ryT x1 ln2_st ln2_mv x2n x2nT h2T
            cx ck hmm relu kk crmm thc cvmm p2 zz ln3_st ln3_mv xx x3 drop x3T_mm x3T lgmm
            r0 r1 rexp rsum rgate rcand ridx oh rankmm ohs rloc8 rloc rkeep rslot rsub rsc sidx
            e_T e_x e_h e_g e_y e_yb e_z e_st e_mv e_norm e_tid""".split()
        for n_ in names:
            s(n_)
        x_in = [sem(f"x_in{c}") for c in range(NCH)]
        e_in = [sem(f"e_in{i}") for i in range(2)]
        scat = [sem(f"scat{i}") for i in range(2)]
        osc = [sem(f"osc{i}") for i in range(2)]
        dout = [sem(f"dout{i}") for i in range(2)]

        STAGES = [("sscan", 2), ("y", 3), ("ln1", 0), ("x1", 3), ("kk", 4), ("delta", 2), ("out", 4),
                  ("mscan", 1), ("route", 4)]
        STEPS = NCH + max(l for _, l in STAGES)

        def run(fns):
            for i in range(STEPS):
                for n_, lag in STAGES:
                    if n_ in fns and 0 <= i - lag < NCH:
                        fns[n_](i - lag)

        def cols(c):
            b, k = divmod(c, CPB)
            return b, k * CH + 1

        block = ctx.enter_context(nc.Block())

        @block.sync
        def _(sp):
            for r, v_ in enumerate((time_decay, time_first, ln1_g, ln1_b, ln2_g, ln2_b)):
                sp.dma_start(vrows[r:r + 1, :], v_.rearrange("(a c) -> a c", a=1)).then_inc(s("v_in"), 16)
            for r, v_ in enumerate((mix_k, mix_v, mix_r, cmix_k, cmix_r)):
                sp.dma_start(vrows[6 + r:7 + r, :], v_.rearrange("a b c -> (a b) c")).then_inc(s("v_in"), 16)
            sp.dma_start(vrows[NVEC:, :], b1.rearrange("e (j p) -> (e j) p", p=P)).then_inc(s("v_in"), 16)
            sp.dma_start(x_sb[:, 0], xf[0]).then_inc(x_in[0], 16)
            for r, w_ in enumerate((w_tk, w_tv, w_tr, w_cr)):
                sp.dma_start(wt_sb[:, r, :], w_).then_inc(s("w_in"), 16)
            sp.dma_start(x_sb[:, 1], xf[1]).then_inc(x_in[1], 16)
            sp.dma_start(wck_sb[:, :], w_ck).then_inc(s("w_in"), 16)
            sp.dma_start(wcv_sb[:, :, :], w_cv.rearrange("(f p) c -> p f c", p=P)).then_inc(s("w_in"), 16)
            sp.dma_start(wg_sb[:, :], wg).then_inc(s("w_in"), 16)
            sp.wait_ge(s("fillset"), 2)
            for e in range(E):
                sp.dma_start(disp_t[e], fill[:, :, :]).then_inc(s("disp_fill"), 16)
            for c in range(2, NCH):
                sp.dma_start(x_sb[:, c], xf[c]).then_inc(x_in[c], 16)
            sp.dma_start(w1_sb[:, :, :], w1.rearrange("e c f -> c e f")).then_inc(s("we_in"), 16)
            for e in range(E):
                sp.dma_start(w2_sb[:, e, :, :], w2[e].rearrange("(f p) c -> p f c", p=P)).then_inc(s("we_in"), 16)
            sp.dma_start(b2_sb[:, :, :], b2.partition_broadcast(P)).then_inc(s("we_in"), 16)
            for c in range(NCH):
                sp.wait_ge(s("drop"), c + 1)
                sp.dma_start(of[c], drp[c % 2][:, :, :]).then_inc(dout[c % 2], 16)
            for e in range(E):
                if e == 0:
                    sp.wait_ge(scat[0], 16 * TPC * NCH // 2)
                    sp.wait_ge(scat[1], 16 * TPC * NCH // 2)
                if e >= 2:
                    sp.wait_ge(s("e_z"), e - 1)
                    sp.wait_ge(s("e_tid"), e - 1)
                sp.dma_start(er[e % 2][:, :, :], disp_t[e]).then_inc(e_in[e % 2], 16)
            sp.wait_ge(dout[0], 16 * NCH // 2)
            sp.wait_ge(dout[1], 16 * NCH // 2)

        W_ATT = 16 * 7
        W_EXP = 16 * (1 + E + 1)

        @block.gpsimd
        def _(pool):
            g = nc.gpsimd
            g.memset(fill[:, :, :], 0.0).then_inc(s("fillset"), 1)
            pool.wait_ge(s("fillset"), 1)
            g.memset(fill[:, :, TOK:TOK + 1], float(4 * N)).then_inc(s("fillset"), 1)
            g.memset(ident[:, :], 0.0).then_inc(s("id0"), 1)
            g.memset(tri[:, :], 1.0).then_inc(s("id0"), 1)
            g.memset(ones[:, :], 1.0).then_inc(s("cst"), 1)
            g.memset(mhalf[:, :], -0.5).then_inc(s("cst"), 1)
            pool.wait_ge(s("id0"), 2)
            g.affine_select(out=ident[:, :], in_=ident[:, :], compare_op=ALU.not_equal, fill=1.0, base=0,
                            pattern=[[-1, P]], channel_multiplier=1).then_inc(s("cst"), 1)
            g.affine_select(out=tri[:, :], in_=tri[:, :], compare_op=ALU.is_gt, fill=0.0, base=0,
                            pattern=[[1, P]], channel_multiplier=-1).then_inc(s("cst"), 1)
            g.iota(iota_e[:, :, :], pattern=[[0, TPC], [1, E]], base=0, channel_multiplier=0,
                   allow_small_or_imprecise_dtypes=True).then_inc(s("cst"), 1)
            g.iota(iota_e8[:, :, :], pattern=[[0, TPC], [1, E]], base=E, channel_multiplier=0,
                   allow_small_or_imprecise_dtypes=True).then_inc(s("cst"), 1)
            g.iota(tokf[:, :, :], pattern=[[CH, NCH], [TILE, TPC]], base=0, channel_multiplier=1,
                   allow_small_or_imprecise_dtypes=True).then_inc(s("cst"), 1)
            step = [0]

            def link(ins):
                step[0] += 1
                ins.then_inc(s("ln_pool"), 1)
                pool.wait_ge(s("ln_pool"), step[0])

            def norm(k, p, mv, src, dst, done):
                w = lnw[:, k, p]
                link(g.tensor_scalar(w[:, 0, :], mv[:, :, 1], 1.0, LN_EPS, ALU.mult, ALU.add))
                link(g.tensor_tensor(w[:, 1, :], w[:, 0, :], mhalf[:, :], ALU.pow))
                link(g.tensor_tensor(w[:, 2, :], mv[:, :, 0], w[:, 1, :], ALU.mult))
                link(g.tensor_scalar(w[:, 3, :], w[:, 2, :], -1.0, 0.0, ALU.mult, ALU.add))
                for j in range(TPC):
                    last = g.tensor_scalar(dst(j), src(j), w[:, 1, j:j + 1], w[:, 3, j:j + 1], ALU.mult, ALU.add)
                last.then_inc(done, 1)

            def ln1(c):
                p = c % 2
                pool.wait_ge(s("ln1_mv"), c + 1)
                if c >= 2:
                    pool.wait_ge(s("xnT"), c - 1)
                norm(0, p, mv1[p], lambda j: x_sb[:, c, j, :], lambda j: xn[p][:, j, :], s("xn"))

            def x1s(c):
                p = c % 2
                pool.wait_ge(s("ln2_mv"), c + 1)
                if c >= 2:
                    pool.wait_ge(s("x2nT"), c - 1)
                norm(1, p, mv2[p], lambda j: x1[p][:, j, :], lambda j: x2n[p][:, j, :], s("x2n"))
                pool.wait_ge(s("xn"), c + 1)
                g.tensor_tensor(x_sb[:, c], x_sb[:, c], x1[p][:, :, :], ALU.add).then_inc(s("xx"), 1)

            def outs(c):
                p = c % 2
                pool.wait_ge(s("ln3_mv"), c + 1)
                if c >= 2:
                    pool.wait_ge(scat[p], 16 * TPC * (c // 2))
                    pool.wait_ge(s("x3T_mm"), c - 1)
                norm(2, p, mv3[p], lambda j: z[p][:, j, :], lambda j: rows[p][:, j, 0:C], s("x3"))
                w = lnw[:, 2, p]
                link(g.tensor_tensor(dsc[:, 0, :], w[:, 1, :], w[:, 1, :], ALU.mult))
                link(g.tensor_tensor(dsc[:, 1, :], dsc[:, 0, :], mv3[p][:, :, 1], ALU.mult))
                link(g.tensor_scalar(dsc[:, 0, :], dsc[:, 1, :], 1.0, LN_EPS, ALU.mult, ALU.add))
                link(g.tensor_tensor(dsc[:, 1, :], dsc[:, 0, :], mhalf[:, :], ALU.pow))
                if c >= 2:
                    pool.wait_ge(dout[p], 16 * (c // 2))
                pool.wait_ge(s("x3"), c + 1)
                for j in range(TPC):
                    last = g.tensor_scalar(drp[p][:, j, :], rows[p][:, j, 0:C], dsc[:, 1, j:j + 1], 0.0,
                                           ALU.mult, ALU.add)
                last.then_inc(s("drop"), 1)

            def route(c):
                p = c % 2
                if c == 0:
                    pool.wait_ge(s("disp_fill"), 16 * E)
                pool.wait_ge(s("rgate"), 2 * c + 2)
                pool.wait_ge(s("sidx"), c + 1)
                for j in range(TPC):
                    g.indirect_dma_start(out=disp[:, :], out_offset=bass.IndirectOffsetOnAxis(ap=sidx[p][:, j:j + 1], axis=0),
                                         in_=rows[p][:, j, :], in_offset=None).then_inc(scat[p], 16)

            run({"ln1": ln1, "x1": x1s, "out": outs, "route": route})

            def send(e):
                p = e % 2
                pool.wait_ge(s("e_norm"), e + 1)
                pool.wait_ge(s("e_tid"), e + 1)
                if e == 0:
                    pool.wait_ge(dout[0], 16 * NCH // 2)
                    pool.wait_ge(dout[1], 16 * NCH // 2)
                for j in range(SPE):
                    g.indirect_dma_start(out=out_rows, out_offset=bass.IndirectOffsetOnAxis(ap=tid[p][:, j:j + 1], axis=0),
                                         in_=xn[p][:, j, :], in_offset=None, bounds_check=N - 1,
                                         oob_is_err=False).then_inc(osc[p], 16)

            for e in range(E):
                p = e % 2
                pool.wait_ge(s("e_mv"), e + 1)
                if e >= 2:
                    pool.wait_ge(osc[p], 16 * SPE * (e // 2))
                norm(0, p, mv1[p], lambda j: z[p][:, j, :], lambda j: xn[p][:, j, :], s("e_norm"))
                send(e)
            pool.wait_ge(osc[0], 16 * SPE * E // 2)
            pool.wait_ge(osc[1], 16 * SPE * E // 2)

        @block.scalar
        def _(act):
            a = nc.scalar

            def ln1(c):
                b, t = cols(c)
                act.wait_ge(s("xnT"), c + 1)
                if c == 0:
                    act.wait_ge(s("vcol"), 1)
                a.activation(hT[:, b, t:t + CH], ps_ta[:, :], ACT.Identity, scale=vcol[:, G1:G1 + 1],
                             bias=vcol[:, B1:B1 + 1]).then_inc(s("hT"), 1)

            def mscan(c):
                p = c % 2
                act.wait_ge(s("efin"), c + 1)
                a.activation(EF[p][:, 0, :], EF[p][:, 0, :], ACT.Exp)
                a.activation(EF[p][:, 1, :], EF[p][:, 1, :], ACT.Exp, scale=-1.0).then_inc(s("efexp"), 1)

            def sscan(c):
                p = c % 2
                act.wait_ge(s("sscan"), c + 1)
                a.activation(LS[p][:, :], Sx[p][:, 0:CH], ACT.Ln).then_inc(s("lns"), 1)

            def delta(c):
                p = c % 2
                act.wait_ge(s("vmm"), c + 1)
                if c >= 2:
                    act.wait_ge(s("y"), c - 1)
                a.activation(V[p][:, :], ps_vr[:, :], ACT.Copy).then_inc(s("v_sb"), 1)
                act.wait_ge(s("abin"), c + 1)
                a.activation(AB[p][:, 0, :], AB[p][:, 0, :], ACT.Exp)
                a.activation(AB[p][:, 1, :], AB[p][:, 1, :], ACT.Exp, scale=-1.0).then_inc(s("abexp"), 1)
                a.activation(TH[p][:, :], LS[p][:, :], ACT.Tanh, scale=0.5, bias=nuh[:, 0:1]).then_inc(s("th"), 1)
                act.wait_ge(s("rmm"), c + 1)
                if c >= 2:
                    act.wait_ge(s("ry"), c - 1)
                a.activation(THR[p][:, :], ps_vr[:, :], ACT.Tanh, scale=0.5).then_inc(s("thr"), 1)

            def x1s(c):
                p = c % 2
                b, t = cols(c)
                act.wait_ge(s("x2nT"), c + 1)
                if c == 0:
                    act.wait_ge(s("hzero"), 2)
                a.activation(h2T[:, b, t:t + CH], ps_ta[:, :], ACT.Identity, scale=vcol[:, G2:G2 + 1],
                             bias=vcol[:, B2:B2 + 1]).then_inc(s("h2T"), 1)
                act.wait_ge(s("h2T"), c + 1)
                if c >= 2:
                    act.wait_ge(s("hmm"), FB * (c - 1))
                a.activation(cx[p][:, :], h2T[:, b, t - 1:t - 1 + CH], ACT.Copy,
                             scale=omix[:, 3:4]).then_inc(s("cx"), 1)

            def kks(c):
                for f in range(FB):
                    n = FB * c + f
                    act.wait_ge(s("hmm"), n + 1)
                    if n >= 2:
                        act.wait_ge(s("kk"), n - 1)
                    a.activation(rl[n % 2][:, :], ps_h[n % 2][:, :], ACT.Relu).then_inc(s("relu"), 1)
                act.wait_ge(s("crmm"), c + 1)
                if c >= 2:
                    act.wait_ge(s("p2"), c - 1)
                a.activation(thc[c % 2][:, :, :].rearrange("p j c -> p (j c)"), ps_cr[:, :], ACT.Tanh,
                             scale=0.5).then_inc(s("thc"), 1)

            def outs(c):
                act.wait_ge(s("x3T_mm"), c + 1)
                if c >= 1:
                    act.wait_ge(s("lgmm"), c)
                a.activation(x3T[:, :], ps_tb[:, :], ACT.Copy).then_inc(s("x3T"), 1)

            def route(c):
                act.wait_ge(s("r1"), c + 1)
                a.activation(ex[:, :, :], lg[:, :, :], ACT.Exp).then_inc(s("rexp"), 1)

            run({"sscan": sscan, "ln1": ln1, "delta": delta, "kk": kks, "mscan": mscan, "out": outs,
                 "x1": x1s, "route": route})

            for e in range(E):
                p = e % 2
                act.wait_ge(s("e_T"), e + 1)
                if e >= 2:
                    act.wait_ge(s("e_h"), FB * (e - 1))
                a.activation(eT[p][:, :], [ps_ta, ps_tb][p][:, :], ACT.Copy).then_inc(s("e_x"), 1)
                if e >= 2:
                    act.wait_ge(s("e_y"), e - 1)
                for f in range(FB):
                    act.wait_ge(s("e_h"), FB * e + f + 1)
                    a.activation(kk[p][:, f, :], ps_h[f % 2][:, :], ACT.Gelu_apprx_tanh,
                                 bias=vcol[:, NVEC + e * FB + f:NVEC + e * FB + f + 1]).then_inc(s("e_g"), 1)

        @block.vector
        def _(dve):
            v = nc.vector
            for b in range(B):
                v.memset(hT[:, b, 0:1], 0.0).then_inc(s("mset"), 1)
            for b in range(B):
                v.memset(h2T[:, b, 0:1], 0.0).then_inc(s("hzero"), 1)
            v.memset(ohs[:, 0, :], 0.0).then_inc(s("ohs"), 1)
            dve.wait_ge(s("vt"), 1)
            v.tensor_copy(vcol[:, :], ps_k[:, 0:NVEC + E * FB]).then_inc(s("vcol"), 1)
            dve.wait_ge(s("vcol"), 1)
            v.tensor_scalar(omix[:, :], vcol[:, MK:MK + 5], -1.0, 1.0, ALU.mult, ALU.add).then_inc(s("wmix"), 1)
            v.tensor_scalar(nuh[:, :], vcol[:, U_:U_ + 1], -0.5, None, ALU.mult).then_inc(s("wmix"), 1)
            dve.wait_ge(s("wmix"), 2)
            dve.wait_ge(s("w_in"), W_ATT)
            for r, m in enumerate((0, 1, 2, 4)):
                v.tensor_scalar(wm_sb[:, r, 0, :], wt_sb[:, r, :], vcol[:, MK + m:MK + m + 1], None, ALU.mult)\
                    .then_inc(s("wmix"), 1)
                v.tensor_scalar(wm_sb[:, r, 1, :], wt_sb[:, r, :], omix[:, m:m + 1], None, ALU.mult)\
                    .then_inc(s("wmix"), 1)

            def stats(c, src, mv, s_st, s_mv):
                for j in range(TPC):
                    last = v.bn_stats(st[c % 2][:, j, :], src(j))
                last.then_inc(s_st, 1)
                dve.wait_ge(s_st, c + 1)
                for j in range(TPC):
                    last = v.bn_aggr(mv[:, j, :], st[c % 2][:, j, :])
                last.then_inc(s_mv, 1)

            def ln1(c):
                dve.wait_ge(x_in[c], 16)
                if c >= 2:
                    dve.wait_ge(s("xn"), c - 1)
                stats(c, lambda j: x_sb[:, c, j, :], mv1[c % 2], s("ln1_st"), s("ln1_mv"))

            def carry(c, buf, init, done):
                if c % CPB == 0:
                    v.memset(buf[c % 2][:, 0:1], init).then_inc(done, 1)
                else:
                    v.tensor_copy(buf[c % 2][:, 0:1], buf[1 - c % 2][:, CH:CH + 1]).then_inc(done, 1)
                dve.wait_ge(done, c + 1)

            def mscan(c):
                p = c % 2
                carry(c, Mx, NEG_INF, s("m0"))
                dve.wait_ge(s("kmm"), c + 1)
                v.tensor_tensor_scan(Mx[p][:, 1:CH + 1], vcol[:, W_:W_ + 1].broadcast_to([P, CH]), ps_k[:, :],
                                     Mx[p][:, 0:1], ALU.add, ALU.max).then_inc(s("mscan"), 1)
                dve.wait_ge(s("mscan"), c + 1)
                v.scalar_tensor_tensor(G[p][:, :], Mx[p][:, 0:CH], vcol[:, W_:W_ + 1], ps_k[:, :],
                                       ALU.add, ALU.subtract).then_inc(s("gdone"), 1)
                dve.wait_ge(s("gdone"), c + 1)
                v.tensor_scalar(EF[p][:, 0, :], G[p][:, :], 0.0, None, ALU.min)
                v.tensor_scalar(EF[p][:, 1, :], G[p][:, :], 0.0, None, ALU.max).then_inc(s("efin"), 1)

            def sscan(c):
                p = c % 2
                carry(c, Sx, 1.0, s("s0"))
                dve.wait_ge(s("efexp"), c + 1)
                v.tensor_tensor_scan(Sx[p][:, 1:CH + 1], EF[p][:, 0, :], EF[p][:, 1, :], Sx[p][:, 0:1],
                                     ALU.mult, ALU.add).then_inc(s("sscan"), 1)

            def delta(c):
                p = c % 2
                dve.wait_ge(s("lns"), c + 1)
                v.tensor_tensor(LS[p][:, :], LS[p][:, :], G[p][:, :], ALU.add).then_inc(s("delta"), 1)
                dve.wait_ge(s("delta"), c + 1)
                v.tensor_scalar(AB[p][:, 0, :], LS[p][:, :], 0.0, None, ALU.min)
                v.tensor_scalar(AB[p][:, 1, :], LS[p][:, :], 0.0, None, ALU.max).then_inc(s("abin"), 1)

            def ys(c):
                p = c % 2
                carry(c, Ax, 0.0, s("a0"))
                dve.wait_ge(s("abexp"), c + 1)
                dve.wait_ge(s("v_sb"), c + 1)
                v.tensor_tensor(AB[p][:, 1, :], AB[p][:, 1, :], V[p][:, :], ALU.mult).then_inc(s("bv"), 1)
                dve.wait_ge(s("bv"), c + 1)
                v.tensor_tensor_scan(Ax[p][:, 1:CH + 1], AB[p][:, 0, :], AB[p][:, 1, :], Ax[p][:, 0:1],
                                     ALU.mult, ALU.add).then_inc(s("ascan"), 1)
                dve.wait_ge(s("ascan"), c + 1)
                if c >= 2:
                    dve.wait_ge(s("ryT"), c - 1)
                v.tensor_tensor(Y[p][:, :], Ax[p][:, 0:CH], V[p][:, :], ALU.subtract).then_inc(s("df"), 1)
                dve.wait_ge(s("df"), c + 1)
                dve.wait_ge(s("th"), c + 1)
                v.scalar_tensor_tensor(Y[p][:, :], TH[p][:, :], 1.0, Y[p][:, :], ALU.add, ALU.mult)\
                    .then_inc(s("q"), 1)
                dve.wait_ge(s("q"), c + 1)
                v.scalar_tensor_tensor(Y[p][:, :], Y[p][:, :], 0.5, V[p][:, :], ALU.mult, ALU.add)\
                    .then_inc(s("y"), 1)
                dve.wait_ge(s("y"), c + 1)
                dve.wait_ge(s("thr"), c + 1)
                v.scalar_tensor_tensor(Y[p][:, :], THR[p][:, :], 1.0, Y[p][:, :], ALU.add, ALU.mult)\
                    .then_inc(s("ry"), 1)

            def x1s(c):
                p = c % 2
                b, t = cols(c)
                dve.wait_ge(s("ryT"), c + 1)
                if c >= 2:
                    dve.wait_ge(s("xx"), c - 1)
                v.scalar_tensor_tensor(x1[p][:, :, :].rearrange("p j c -> p (j c)"), ps_tb[:, :], 0.5,
                                       x_sb[:, c].rearrange("p j c -> p (j c)"), ALU.mult, ALU.add)\
                    .then_inc(s("x1"), 1)
                dve.wait_ge(s("x1"), c + 1)
                if c >= 2:
                    dve.wait_ge(s("x2n"), c - 1)
                stats(c, lambda j: x1[p][:, j, :], mv2[p], s("ln2_st"), s("ln2_mv"))

            def kks(c):
                p = c % 2
                b, t = cols(c)
                dve.wait_ge(s("cx"), c + 1)
                v.scalar_tensor_tensor(cx[p][:, :], h2T[:, b, t:t + CH], vcol[:, CK:CK + 1], cx[p][:, :],
                                       ALU.mult, ALU.add).then_inc(s("ck"), 1)
                if c >= 2:
                    dve.wait_ge(s("cvmm"), c - 1)
                for f in range(FB):
                    n = FB * c + f
                    dve.wait_ge(s("relu"), n + 1)
                    v.tensor_tensor(kk[p][:, f, :], ps_h[n % 2][:, :], rl[n % 2][:, :], ALU.mult)\
                        .then_inc(s("kk"), 1)

            def outs(c):
                p = c % 2
                dve.wait_ge(s("cvmm"), c + 1)
                dve.wait_ge(s("thc"), c + 1)
                if c >= 2:
                    dve.wait_ge(s("x3"), c - 1)
                zf = z[p][:, :, :].rearrange("p j c -> p (j c)")
                v.scalar_tensor_tensor(zf, thc[p][:, :, :].rearrange("p j c -> p (j c)"), 1.0, ps_cv[:, :],
                                       ALU.add, ALU.mult).then_inc(s("p2"), 1)
                dve.wait_ge(s("p2"), c + 1)
                dve.wait_ge(s("xx"), c + 1)
                v.scalar_tensor_tensor(zf, zf, 0.5, x_sb[:, c].rearrange("p j c -> p (j c)"),
                                       ALU.mult, ALU.add).then_inc(s("zz"), 1)
                dve.wait_ge(s("zz"), c + 1)
                if c >= 2:
                    dve.wait_ge(s("drop"), c - 1)
                stats(c, lambda j: z[p][:, j, :], mv3[p], s("ln3_st"), s("ln3_mv"))

            def route(c):
                p = c % 2
                lps = ps_cr[:, 0:TPC * E].rearrange("p (j e) -> p j e", e=E)
                rps = ps_cr[:, TPC * E:2 * TPC * E].rearrange("p (j e) -> p j e", e=E)

                def wide(t):
                    return t.unsqueeze(2).broadcast_to([P, TPC, E])

                dve.wait_ge(s("lgmm"), c + 1)
                v.tensor_reduce(mx[:, :], lps, AX.X, ALU.max).then_inc(s("r0"), 1)
                dve.wait_ge(s("r0"), c + 1)
                v.tensor_tensor(lg[:, :, :], lps, wide(mx[:, :]), ALU.subtract).then_inc(s("r1"), 1)
                dve.wait_ge(s("r1"), c + 1)
                v.tensor_scalar(cand[:, :, :], lg[:, :, :], 0.0, -float(E), ALU.is_equal, ALU.mult)\
                    .then_inc(s("rcand"), 1)
                dve.wait_ge(s("rcand"), 2 * c + 1)
                v.tensor_tensor(cand[:, :, :], cand[:, :, :], iota_e8[:, :, :], ALU.add).then_inc(s("rcand"), 1)
                dve.wait_ge(s("rcand"), 2 * c + 2)
                v.tensor_reduce(eidx[:, :], cand[:, :, :], AX.X, ALU.min).then_inc(s("ridx"), 1)
                dve.wait_ge(s("ridx"), c + 1)
                v.tensor_tensor(oh[:, :, :], iota_e[:, :, :], wide(eidx[:, :]), ALU.is_equal).then_inc(s("oh"), 1)
                dve.wait_ge(s("rexp"), c + 1)
                v.tensor_reduce(sm[:, :], ex[:, :, :], AX.X, ALU.add).then_inc(s("rsum"), 1)
                dve.wait_ge(s("rsum"), c + 1)
                dve.wait_ge(s("x3"), c + 1)
                v.reciprocal(rows[p][:, :, GATE], sm[:, :]).then_inc(s("rgate"), 1)
                v.tensor_copy(rows[p][:, :, TOK], tokf[:, c, :]).then_inc(s("rgate"), 1)
                dve.wait_ge(s("oh"), c + 1)
                v.tensor_reduce(ohr[:, :], oh[:, :, :].rearrange("p j e -> p e j"), AX.X, ALU.add)\
                    .then_inc(s("rloc8"), 1)
                dve.wait_ge(s("rloc8"), 2 * c + 1)
                v.tensor_tensor(ohs[:, 1 - p, :], ohs[:, p, :], ohr[:, :], ALU.add).then_inc(s("ohs"), 1)
                dve.wait_ge(s("rankmm"), c + 1)
                v.tensor_tensor(loc8[:, :, :], rps, oh[:, :, :], ALU.mult).then_inc(s("rloc8"), 1)
                dve.wait_ge(s("rloc8"), 2 * c + 2)
                v.tensor_reduce(loc[:, :], loc8[:, :, :], AX.X, ALU.add).then_inc(s("rloc"), 1)
                dve.wait_ge(s("rloc"), c + 1)
                v.tensor_scalar(keep[:, :], loc[:, :], float(CAP), None, ALU.is_lt).then_inc(s("rkeep"), 1)
                v.scalar_tensor_tensor(slot[:, :], eidx[:, :], float(CAP), loc[:, :], ALU.mult, ALU.add)\
                    .then_inc(s("rslot"), 1)
                dve.wait_ge(s("rslot"), c + 1)
                v.scalar_tensor_tensor(slot[:, :], slot[:, :], -float(TRASH), tokf[:, c, :], ALU.add, ALU.subtract)\
                    .then_inc(s("rsub"), 1)
                dve.wait_ge(s("rsub"), c + 1)
                v.tensor_tensor(slot[:, :], slot[:, :], keep[:, :], ALU.mult).then_inc(s("rsc"), 1)
                dve.wait_ge(s("rsc"), c + 1)
                if c >= 2:
                    dve.wait_ge(scat[p], 16 * TPC * (c // 2))
                v.scalar_tensor_tensor(sidx[p][:, :], slot[:, :], float(TRASH), tokf[:, c, :], ALU.add, ALU.add)\
                    .then_inc(s("sidx"), 1)

            run({"sscan": sscan, "ln1": ln1, "delta": delta, "kk": kks, "mscan": mscan, "y": ys,
                 "out": outs, "x1": x1s, "route": route})

            for e in range(E):
                p = e % 2
                dve.wait_ge(e_in[p], 16 * (e // 2 + 1))
                if e >= 2:
                    dve.wait_ge(osc[p], 16 * SPE * (e // 2))
                v.tensor_copy(tid[p][:, :], er[p][:, :, TOK]).then_inc(s("e_tid"), 1)
                if e == 0:
                    dve.wait_ge(s("we_in"), W_EXP)
                dve.wait_ge(s("e_y"), e + 1)
                dve.wait_ge(s("drop") if e < 2 else s("e_norm"), NCH if e < 2 else e - 1)
                yb = [ps_cv, ps_cr][p][:, :].rearrange("p (j c) -> p j c", c=C)
                v.tensor_tensor(z[p][:, :, :], yb, b2_sb[:, e:e + 1, :].broadcast_to([P, SPE, C]), ALU.add)\
                    .then_inc(s("e_yb"), 1)
                dve.wait_ge(s("e_yb"), e + 1)
                for j in range(SPE):
                    last = v.scalar_tensor_tensor(z[p][:, j, :], z[p][:, j, :], er[p][:, j, GATE:GATE + 1],
                                                  er[p][:, j, 0:C], ALU.mult, ALU.add)
                last.then_inc(s("e_z"), 1)
                dve.wait_ge(s("e_z"), e + 1)
                stats(e, lambda j: z[p][:, j, :], mv1[p], s("e_st"), s("e_mv"))

        @block.tensor
        def _(pe):
            t_ = nc.tensor
            NV = NVEC + E * FB
            pe.wait_ge(s("cst"), 7)
            pe.wait_ge(s("v_in"), 16 * 12)
            t_.transpose(ps_k[:, 0:NV], vrows[:, :], ident[0:NV, 0:NV]).then_inc(s("vt"), 1)
            pe.wait_ge(s("wmix"), 10)
            pe.wait_ge(s("mset"), B)

            def turn(dst, src, done):
                for j in range(TPC):
                    last = t_.transpose(dst[:, j * TILE:(j + 1) * TILE], src(j), ident[:, :])
                last.then_inc(done, 1)

            def mixed(dst, r, b, t, done):
                t_.matmul(dst[:, :], wm_sb[:, r, 0, :], hT[:, b, t:t + CH], start=True, stop=False)
                t_.matmul(dst[:, :], wm_sb[:, r, 1, :], hT[:, b, t - 1:t - 1 + CH], start=False, stop=True)\
                    .then_inc(done, 1)

            def ln1(c):
                pe.wait_ge(s("xn"), c + 1)
                if c >= 1:
                    pe.wait_ge(s("hT"), c)
                if c >= 4:
                    pe.wait_ge(s("h2T"), c - 3)
                turn(ps_ta, lambda j: xn[c % 2][:, j, :], s("xnT"))

            def mscan(c):
                b, t = cols(c)
                pe.wait_ge(s("hT"), c + 1)
                if c >= 1:
                    pe.wait_ge(s("gdone"), c)
                mixed(ps_k, 0, b, t, s("kmm"))

            def delta(c):
                b, t = cols(c)
                if c >= 1:
                    pe.wait_ge(s("thr"), c)
                mixed(ps_vr, 1, b, t, s("vmm"))
                pe.wait_ge(s("v_sb"), c + 1)
                mixed(ps_vr, 2, b, t, s("rmm"))

            def ys(c):
                pe.wait_ge(s("ry"), c + 1)
                if c >= 1:
                    pe.wait_ge(s("x1"), c)
                if c >= 2:
                    pe.wait_ge(s("x3T"), c - 1)
                turn(ps_tb, lambda j: Y[c % 2][:, j * TILE:(j + 1) * TILE], s("ryT"))

            def x1s(c):
                pe.wait_ge(s("x2n"), c + 1)
                pe.wait_ge(s("hT"), min(c + 4, NCH))
                turn(ps_ta, lambda j: x2n[c % 2][:, j, :], s("x2nT"))

            def kks(c):
                p = c % 2
                b, t = cols(c)
                pe.wait_ge(s("ck"), c + 1)
                for f in range(FB):
                    n = FB * c + f
                    if n >= 2:
                        pe.wait_ge(s("kk"), n - 1)
                    t_.matmul(ps_h[n % 2][:, :], wck_sb[:, f * P:(f + 1) * P], cx[p][:, :], start=True, stop=True)\
                        .then_inc(s("hmm"), 1)
                if c >= 1:
                    pe.wait_ge(s("rloc8"), 2 * c)
                for j in range(TPC):
                    o = ps_cr[:, j * C:(j + 1) * C]
                    a_ = t + j * TILE
                    t_.matmul(o, h2T[:, b, a_:a_ + TILE], wm_sb[:, 3, 0, :], start=True, stop=False)
                    last = t_.matmul(o, h2T[:, b, a_ - 1:a_ - 1 + TILE], wm_sb[:, 3, 1, :], start=False, stop=True)
                last.then_inc(s("crmm"), 1)
                pe.wait_ge(s("kk"), FB * (c + 1))
                if c >= 1:
                    pe.wait_ge(s("p2"), c)
                for j in range(TPC):
                    for f in range(FB):
                        last = t_.matmul(ps_cv[:, j * C:(j + 1) * C], kk[p][:, f, j * TILE:(j + 1) * TILE],
                                         wcv_sb[:, f, :], start=(f == 0), stop=(f == FB - 1))
                last.then_inc(s("cvmm"), 1)

            def outs(c):
                pe.wait_ge(s("x3"), c + 1)
                pe.wait_ge(s("x1"), min(c + 2, NCH))
                turn(ps_tb, lambda j: rows[c % 2][:, j, 0:C], s("x3T_mm"))
                pe.wait_ge(s("x3T"), c + 1)
                pe.wait_ge(s("thc"), c + 1)
                for j in range(TPC):
                    last = t_.matmul(ps_cr[:, j * E:(j + 1) * E], x3T[:, j * TILE:(j + 1) * TILE], wg_sb[:, :],
                                     start=True, stop=True)
                last.then_inc(s("lgmm"), 1)

            def route(c):
                R = TPC * E
                pe.wait_ge(s("oh"), c + 1)
                pe.wait_ge(s("ohs"), c + 1)
                ohf = oh[:, :, :].rearrange("p j e -> p (j e)")
                t_.matmul(ps_cr[:, R:2 * R], tri[:, :], ohf, start=True, stop=False)
                t_.matmul(ps_cr[:, R:2 * R].rearrange("p (j e) -> p j e", e=E), ones[:, :],
                          ohs[:, c % 2:c % 2 + 1, :].broadcast_to([P, TPC, E]), start=False, stop=False)
                for i in range(TPC - 1):
                    last = t_.matmul(ps_cr[:, R + (i + 1) * E:2 * R].rearrange("p (j e) -> p j e", e=E), ones[:, :],
                                     oh[:, i:i + 1, :].broadcast_to([P, TPC - 1 - i, E]),
                                     start=False, stop=(i == TPC - 2))
                last.then_inc(s("rankmm"), 1)

            run({"ln1": ln1, "delta": delta, "kk": kks, "mscan": mscan, "y": ys, "out": outs,
                 "x1": x1s, "route": route})

            pe.wait_ge(s("we_in"), W_EXP)

            def second(e):
                p = e % 2
                pe.wait_ge(s("e_g"), FB * (e + 1))
                if e >= 2:
                    pe.wait_ge(s("e_yb"), e - 1)
                if e == 1:
                    pe.wait_ge(s("rloc8"), 2 * NCH)
                for j in range(SPE):
                    for f in range(FB):
                        last = t_.matmul([ps_cv, ps_cr][p][:, j * C:(j + 1) * C], kk[p][:, f, j * TILE:(j + 1) * TILE],
                                         w2_sb[:, e, f, :], start=(f == 0), stop=(f == FB - 1))
                last.then_inc(s("e_y"), 1)

            for e in range(E):
                p = e % 2
                pe.wait_ge(e_in[p], 16 * (e // 2 + 1))
                if e >= 2:
                    pe.wait_ge(s("e_x"), e - 1)
                turn([ps_ta, ps_tb][p], lambda j: er[p][:, j, 0:C], s("e_T"))
                pe.wait_ge(s("e_x"), e + 1)
                for f in range(FB):
                    n = FB * e + f
                    if n >= 2:
                        pe.wait_ge(s("e_g"), n - 1)
                    t_.matmul(ps_h[f % 2][:, :], w1_sb[:, e, f * P:(f + 1) * P], eT[p][:, :], start=True, stop=True)\
                        .then_inc(s("e_h"), 1)
                if e >= 1:
                    second(e - 1)
            second(E - 1)


_INS = ['L0_attn_x', 'L0_attn_time_decay', 'L0_attn_time_first', 'L0_attn_w_tk', 'L0_attn_w_tv', 'L0_attn_w_tr',
        'L0_attn_w_ck', 'L0_attn_w_cv', 'L0_attn_w_cr', 'L0_attn_ln1_g', 'L0_attn_ln1_b', 'L0_attn_ln2_g',
        'L0_attn_ln2_b', 'L0_attn_mix_k', 'L0_attn_mix_v', 'L0_attn_mix_r', 'L0_attn_cmix_k', 'L0_attn_cmix_r',
        'L0_ffn_wg', 'L0_ffn_w1', 'L0_ffn_b1', 'L0_ffn_w2', 'L0_ffn_b2']
_OUTS = [((2, 2048, 128), 'float32')]


def kernel(**inputs):
    import numpy as _np
    import concourse.bacc as _bacc
    from concourse import mybir as _mybir
    from concourse.bass_utils import run_bass_kernel_spmd as _run

    nc = _bacc.Bacc("TRN2", target_bir_lowering=False, num_devices=1)
    arrays, args = {}, []
    for name in _INS:
        a = _np.ascontiguousarray(inputs[name])
        arrays[f"in_{name}_dram"] = a
        args.append(nc.dram_tensor(f"in_{name}_dram", a.shape, _mybir.dt.from_np(a.dtype), kind="ExternalInput").ap())
    for i, (shape, dtype) in enumerate(_OUTS):
        dt = _mybir.dt.from_np(_np.dtype(dtype))
        args.append(nc.dram_tensor(f"out_{i}_dram", shape, dt, kind="ExternalOutput").ap())
    rwkv_moe_kernel(nc, *args)
    r = _run(nc, [arrays], core_ids=[0])
    return r.results[0]["out_0_dram"]
```

```python
from contextlib import ExitStack

import concourse.bass as bass
from concourse import mybir

ALU = mybir.AluOpType
ACT = mybir.ActivationFunctionType
AX = mybir.AxisListType
F32 = mybir.dt.float32
BF16 = mybir.dt.bfloat16
U32 = mybir.dt.uint32

P = 128
LN_EPS = 1e-05
NEG_INF = -1e38
BIG = 3e38
W_, U_, G1, B1, G2, B2, MK, MV, MR, CK, CR = range(11)
NVEC = 11


def rwkv_moe_kernel(nc, x, time_decay, time_first, w_tk, w_tv, w_tr, w_ck, w_cv, w_cr,
                    ln1_g, ln1_b, ln2_g, ln2_b, mix_k, mix_v, mix_r, cmix_k, cmix_r,
                    wg, w1, b1, w2, b2, out):
    B, T, C = x.shape
    E, _, F = w1.shape
    N = B * T
    TILE = P
    CH = 512
    TPC = CH // TILE
    NCH = N // CH
    CPB = T // CH
    FB = F // P
    CAP = (N + E - 1) // E
    SPE = CAP // TILE
    ROW = C + 2
    GATE, TOK = C, C + 1
    assert C == P and CAP == CH and F == 4 * P

    xf = x.rearrange("b (k j p) c -> (b k) p j c", p=TILE, j=TPC)
    of = out.rearrange("b (k j p) c -> (b k) p j c", p=TILE, j=TPC)
    out_rows = out.rearrange("b t c -> (b t) c")
    disp = nc.dram_tensor("disp", [E * CAP, ROW], F32, kind="Internal").ap()
    disp_t = disp[:, :].rearrange("(e j p) r -> e p j r", p=TILE, j=SPE)

    with ExitStack() as ctx:
        def sb(name, shape, dt=F32):
            return ctx.enter_context(nc.sbuf_tensor(name, shape, dt))

        def sem(name):
            return ctx.enter_context(nc.semaphore(name))

        def bank(name):
            return ctx.enter_context(nc.psum_tensor(name, [P, 512], F32))

        ps_k, ps_vr, ps_ta, ps_tb = bank("ps_k"), bank("ps_vr"), bank("ps_ta"), bank("ps_tb")
        ps_h = [bank("ps_h0"), bank("ps_h1")]
        ps_cv, ps_cr = bank("ps_cv"), bank("ps_cr")
        ps_e = [ps_h[0], ps_h[1], ps_k, ps_vr]

        x_raw = sb("x_raw", [P, E * SPE * ROW])
        x_sb = x_raw[:, 0:N // P * C].rearrange("p (k j c) -> p k j c", j=TPC, c=C)
        er = x_raw[:, :].rearrange("p (e j r) -> p e j r", j=SPE, r=ROW)
        vrows = sb("vrows", [NVEC + E * FB, P])
        vcol = sb("vcol", [P, NVEC + E * FB])
        wt_sb = sb("wt_sb", [P, 4, C])
        wm_sb = sb("wm_sb", [P, 4, 2, C])
        wck_sb = sb("wck_sb", [P, F])
        wcv_sb = sb("wcv_sb", [P, FB, C])
        wg_sb = sb("wg_sb", [P, E])
        w1_sb = sb("w1_sb", [P, E, F])
        w2_sb = sb("w2_sb", [P, E, FB, C])
        b2_sb = sb("b2_sb", [P, E, C])
        ident = sb("ident", [P, P])
        tri = sb("tri", [P, P], BF16)
        ones = sb("ones", [P, P], BF16)
        mhalf = sb("mhalf", [P, TPC])
        iota_m = sb("iota_m", [P, TPC, E])
        omix = sb("omix", [P, 5])
        nuh = sb("nuh", [P, 1])
        fill = sb("fill", [P, SPE, ROW])
        rows = sb("rows", [P, NCH, TPC, ROW])
        mv3 = sb("mv3", [P, NCH, TPC, 2])
        rs3 = sb("rs3", [P, NCH, TPC])
        zero = sb("zero", [P, 1])
        def two(name, shape, dt=F32):
            return [sb(f"{name}{i}", shape, dt) for i in range(2)]

        hT, h2T = two("hT", [P, CH + 1]), two("h2T", [P, CH + 1])
        mv1, mv2 = two("mv1", [P, TPC, 2]), two("mv2", [P, TPC, 2])
        st = two("st", [P, TPC, 6])
        lnw = sb("lnw", [P, 3, 2, TPC])
        nmr = sb("nmr", [P, 2, 2, 2, TPC])
        rs = sb("rs", [P, 2, 2, TPC])
        xn = two("xn", [P, TPC, C])
        Mx = two("Mx", [P, CH + 1])
        Sx = two("Sx", [P, CH + 1])
        Ax = two("Ax", [P, CH + 1])
        G = two("G", [P, CH])
        EF = two("EF", [P, 2, CH])
        LS = two("LS", [P, CH])
        AB = two("AB", [P, 2, CH])
        V = two("V", [P, CH])
        TH = two("TH", [P, CH])
        THR = two("THR", [P, CH])
        Y = two("Y", [P, CH])
        x1 = two("x1", [P, TPC, C])
        x2n = two("x2n", [P, TPC, C])
        cx = two("cx", [P, CH])
        rl = two("rl", [P, CH])
        kk = two("kk", [P, FB, CH])
        thc = two("thc", [P, TPC, C])
        z = two("z", [P, TPC, C])
        dsc = two("dsc", [P, 3, TPC])
        x3T = sb("x3T", [P, CH])
        mx = sb("mx", [P, TPC])
        lg = sb("lg", [P, TPC, E])
        ex = sb("ex", [P, TPC, E])
        sm = sb("sm", [P, TPC])
        cand = sb("cand", [P, TPC, E])
        eidx = sb("eidx", [P, TPC])
        oh = sb("oh", [P, TPC, E], BF16)
        ohs = sb("ohs", [P, 2, E], BF16)
        ohr = sb("ohr", [P, E])
        loc8 = sb("loc8", [P, TPC, E])
        loc = sb("loc", [P, TPC])
        pen = sb("pen", [P, TPC])
        slot = sb("slot", [P, TPC])
        sidx = two("sidx", [P, TPC], U32)
        eT = V
        tid = sb("tid", [P, E, SPE], U32)
        eo = [xn[0], xn[1], x2n[0], x2n[1]]
        NEO = 4

        S = {}

        def s(name):
            if name not in S:
                S[name] = sem(name)
            return S[name]

        names = """th0 h0 h20 rst3 kkd kka relu0 relu1 eclamp e_rst w_in we_in v_in vt vcol cst id0 fillset disp_fill out_drop wmix zset
            ln1_st ln1_mv ln_pool xn xnT hT kmm vmm rmm m0 mscan gdone efin efexp s0 sscan lns
            delta abin abexp th v_sb thr bv a0 ascan df q y ry ryT x1 ln2_st ln2_mv x2n x2nT h2T
            cx ck hmm relu kk crmm thc cvmm p2 zz ln3_st ln3_mv xx x3 drop x3T_mm x3T lgmm
            r0 r1 rexp rsum rgate rcand ridx oh rankmm ohs rloc8 rloc rkeep rslot rsub rsc sidx
            e_T e_x e_h e_g e_y e_yb e_z e_st e_mv e_norm e_tid""".split()
        for n_ in names:
            s(n_)
        x_in = [sem(f"x_in{c}") for c in range(NCH)]
        e_in = [sem(f"e_in{e}") for e in range(E)]
        scat = [sem(f"scat{c}") for c in range(NCH)]
        osc = [sem(f"osc{i}") for i in range(4)]
        dout = sem("dout")

        AT = dict(ln1=0.525, kmm=0.675, m=1.047, vmm=1.402, s=1.564, d=1.797, y1=2.539, y2=2.652, x1=2.774, cr=3.194,
                  ck=3.394, cv=3.744, z=4.221, n3=4.474, r1=4.702, r2=5.032, drop=12.894)
        ORDER = sorted((c + at, n, c) for n, (s_, at) in enumerate(AT.items()) for c in range(NCH))
        STAGES = list(AT)

        def run(fns):
            for _, n, c in ORDER:
                if STAGES[n] in fns:
                    fns[STAGES[n]](c)

        def before(stage, at, c):
            here = (c + AT[at], STAGES.index(at))
            return sum((k + AT[stage], STAGES.index(stage)) < here for k in range(NCH))

        def freed(eng, at, c, *users):
            for stage, read in users:
                n = before(stage, at, c)
                if n:
                    eng.wait_ge(read, n)

        def deltas(c):
            return c + 1 + c // CPB + 1

        block = ctx.enter_context(nc.Block())

        @block.sync
        def _(sp):
            sp.dma_start(x_sb[:, 0], xf[0]).then_inc(x_in[0], 16)
            for r, v_ in enumerate((mix_k, mix_v, mix_r, cmix_k, cmix_r)):
                sp.dma_start(vrows[6 + r:7 + r, :], v_.rearrange("a b c -> (a b) c")).then_inc(s("v_in"), 16)
            for r, w_ in enumerate((w_tk, w_tv, w_tr, w_cr)):
                sp.dma_start(wt_sb[:, r, :], w_).then_inc(s("w_in"), 16)
            sp.dma_start(x_sb[:, 1], xf[1]).then_inc(x_in[1], 16)
            sp.dma_start(wck_sb[:, :], w_ck).then_inc(s("w_in"), 16)
            sp.dma_start(wcv_sb[:, :, :], w_cv.rearrange("(f p) c -> p f c", p=P)).then_inc(s("w_in"), 16)
            sp.dma_start(wg_sb[:, :], wg).then_inc(s("w_in"), 16)
            sp.dma_start(x_sb[:, 2], xf[2]).then_inc(x_in[2], 16)
            sp.wait_ge(s("fillset"), 2)
            for e in range(E):
                sp.dma_start(disp_t[e], fill[:, :, :]).then_inc(s("disp_fill"), 16)
            for c in range(3, NCH):
                sp.dma_start(x_sb[:, c], xf[c]).then_inc(x_in[c], 16)
            sp.dma_start(w1_sb[:, :, :], w1.rearrange("e c f -> c e f")).then_inc(s("we_in"), 16)
            for e in range(E):
                sp.dma_start(w2_sb[:, e, :, :], w2[e].rearrange("(f p) c -> p f c", p=P)).then_inc(s("we_in"), 16)
            sp.dma_start(b2_sb[:, :, :], b2.partition_broadcast(P)).then_inc(s("we_in"), 16)
            for c in range(NCH):
                sp.wait_ge(scat[c], 16 * TPC)
            for e in range(E):
                sp.dma_start(er[:, e], disp_t[e]).then_inc(e_in[e], 16)
            for c in range(NCH):
                sp.wait_ge(s("drop"), c + 1)
                sp.dma_start(of[c], rows[:, c, :, 0:C]).then_inc(dout, 16)
            sp.wait_ge(dout, 16 * NCH)

        W_ATT = 16 * 7
        W_EXP = 16 * (1 + E + 1)

        @block.gpsimd
        def _(pool):
            g = nc.gpsimd
            g.memset(fill[:, :, :], 0.0).then_inc(s("fillset"), 1)
            pool.wait_ge(s("fillset"), 1)
            g.memset(fill[:, :, TOK:TOK + 1], float(4 * N)).then_inc(s("fillset"), 1)
            g.memset(ident[:, :], 0.0).then_inc(s("id0"), 1)
            g.memset(tri[:, :], 1.0).then_inc(s("id0"), 1)
            g.memset(ones[:, :], 1.0).then_inc(s("cst"), 1)
            g.memset(mhalf[:, :], -0.5).then_inc(s("cst"), 1)
            pool.wait_ge(s("id0"), 2)
            g.affine_select(out=ident[:, :], in_=ident[:, :], compare_op=ALU.not_equal, fill=1.0, base=0,
                            pattern=[[-1, P]], channel_multiplier=1).then_inc(s("cst"), 1)
            g.affine_select(out=tri[:, :], in_=tri[:, :], compare_op=ALU.is_gt, fill=0.0, base=0,
                            pattern=[[1, P]], channel_multiplier=-1).then_inc(s("cst"), 1)
            g.iota(iota_m[:, :, :], pattern=[[0, TPC], [1, E]], base=-E, channel_multiplier=0,
                   allow_small_or_imprecise_dtypes=True).then_inc(s("cst"), 1)
            g.iota(rows[:, :, :, TOK], pattern=[[CH, NCH], [TILE, TPC]], base=0, channel_multiplier=1,
                   allow_small_or_imprecise_dtypes=True).then_inc(s("cst"), 1)
            step = [0]

            def link(ins):
                step[0] += 1
                ins.then_inc(s("ln_pool"), 1)
                pool.wait_ge(s("ln_pool"), step[0])

            def rstd(k, p, mv, dst, done=None):
                w = lnw[:, k, p, :]
                link(g.tensor_scalar(w, mv[:, :, 1], 1.0, LN_EPS, ALU.mult, ALU.add))
                last = g.tensor_tensor(dst, w, mhalf[:, :], ALU.pow)
                if done is None:
                    link(last)
                else:
                    last.then_inc(done, 1)

            def norm(k, p, mv, src, dst, done):
                g.tensor_scalar(nmr[:, k, p, 0, :], mv[:, :, 0], -1.0, 0.0, ALU.mult, ALU.add)
                rstd(k, p, mv, rs[:, k, p, :])
                link(g.tensor_tensor(nmr[:, k, p, 1, :], nmr[:, k, p, 0, :], rs[:, k, p, :], ALU.mult))
                for j in range(TPC):
                    last = g.tensor_scalar(dst(j), src(j), rs[:, k, p, j:j + 1], nmr[:, k, p, 1, j:j + 1],
                                           ALU.mult, ALU.add)
                last.then_inc(done, 1)

            def ln1(c):
                p = c % 2
                if c == 0:
                    pool.wait_ge(s("cst"), 6)
                pool.wait_ge(s("ln1_mv"), c + 1)
                if c >= 2:
                    pool.wait_ge(s("xnT"), c - 1)
                norm(0, p, mv1[p], lambda j: x_sb[:, c, j, :], lambda j: xn[p][:, j, :], s("xn"))

            def x1s(c):
                p = c % 2
                pool.wait_ge(s("ln2_mv"), c + 1)
                if c >= 2:
                    pool.wait_ge(s("x2nT"), c - 1)
                norm(1, p, mv2[p], lambda j: x1[p][:, j, :], lambda j: x2n[p][:, j, :], s("x2n"))
                pool.wait_ge(s("xn"), c + 1)
                g.tensor_tensor(x_sb[:, c], x_sb[:, c], x1[p][:, :, :], ALU.add).then_inc(s("xx"), 1)

            def zs(c):
                pool.wait_ge(s("ln3_mv"), c + 1)
                rstd(2, c % 2, mv3[:, c], rs3[:, c, :], s("rst3"))

            def r2(c):
                p = c % 2
                if c == 0:
                    pool.wait_ge(s("disp_fill"), 16 * E)
                    pool.wait_ge(s("cst"), 6)
                pool.wait_ge(s("rgate"), c + 1)
                pool.wait_ge(s("sidx"), c + 1)
                for j in range(TPC):
                    g.indirect_dma_start(out=disp[:, :], out_offset=bass.IndirectOffsetOnAxis(ap=sidx[p][:, j:j + 1], axis=0),
                                         in_=rows[:, c, j, :], in_offset=None, bounds_check=E * CAP - 1,
                                         oob_is_err=False).then_inc(scat[c], 16)

            def drop(c):
                d = dsc[c % 2]
                pool.wait_ge(s("rst3"), c + 1)
                link(g.tensor_tensor(d[:, 0, :], rs3[:, c, :], rs3[:, c, :], ALU.mult))
                link(g.tensor_tensor(d[:, 1, :], d[:, 0, :], mv3[:, c, :, 1], ALU.mult))
                link(g.tensor_scalar(d[:, 0, :], d[:, 1, :], 1.0, LN_EPS, ALU.mult, ALU.add))
                link(g.tensor_tensor(d[:, 2, :], d[:, 0, :], mhalf[:, :], ALU.pow))
                pool.wait_ge(scat[c], 16 * TPC)
                for j in range(TPC):
                    last = g.tensor_scalar(rows[:, c, j, 0:C], rows[:, c, j, 0:C], d[:, 2, j:j + 1], 0.0,
                                           ALU.mult, ALU.add)
                last.then_inc(s("drop"), 1)

            run({"ln1": ln1, "x1": x1s, "z": zs, "r2": r2, "drop": drop})

            def send(e):
                if e == 0:
                    pool.wait_ge(dout, 16 * NCH)
                pool.wait_ge(s("e_norm"), e + 1)
                for j in range(SPE):
                    g.indirect_dma_start(out=out_rows, out_offset=bass.IndirectOffsetOnAxis(ap=tid[:, e, j:j + 1], axis=0),
                                         in_=eo[e % NEO][:, j, :], in_offset=None, bounds_check=N - 1,
                                         oob_is_err=False).then_inc(osc[e % NEO], 16)

            for e in range(E):
                pool.wait_ge(s("e_mv"), e + 1)
                if e >= 2:
                    pool.wait_ge(s("e_norm"), e - 1)
                rstd(0, e % 2, mv1[e % 2], rs[:, 0, e % 2, :], s("e_rst"))
                if e >= 1:
                    send(e - 1)
            send(E - 1)
            for i in range(NEO):
                pool.wait_ge(osc[i], 16 * SPE * E // NEO)

        @block.scalar
        def _(act):
            a = nc.scalar
            for r, v_ in enumerate((time_decay, time_first, ln1_g, ln1_b, ln2_g, ln2_b)):
                act.dma_start(vrows[r:r + 1, :], v_.rearrange("(a c) -> a c", a=1)).then_inc(s("v_in"), 16)
            act.dma_start(vrows[NVEC:, :], b1.rearrange("e (j p) -> (e j) p", p=P)).then_inc(s("v_in"), 16)

            def before_chunk(c, buf, written, read, per, done):
                p = c % 2
                if c >= 2:
                    act.wait_ge(read, per * (c - 1))
                if c % CPB == 0:
                    src = zero[:, 0:1]
                else:
                    src = buf[1 - p][:, CH:CH + 1]
                    act.wait_ge(written, c)
                a.activation(buf[p][:, 0:1], src, ACT.Copy).then_inc(done, 1)

            def ln1(c):
                p = c % 2
                if c == 0:
                    act.wait_ge(s("vcol"), 1)
                    act.wait_ge(s("zset"), 1)
                before_chunk(c, hT, s("hT"), s("rmm"), 1, s("h0"))
                act.wait_ge(s("xnT"), c + 1)
                a.activation(hT[p][:, 1:CH + 1], ps_ta[:, :], ACT.Identity, scale=vcol[:, G1:G1 + 1],
                             bias=vcol[:, B1:B1 + 1]).then_inc(s("hT"), 1)

            def mscan(c):
                p = c % 2
                act.wait_ge(s("efin"), c + 1)
                a.activation(EF[p][:, 0, :], EF[p][:, 0, :], ACT.Exp)
                a.activation(EF[p][:, 1, :], EF[p][:, 1, :], ACT.Exp, scale=-1.0).then_inc(s("efexp"), 1)

            def sscan(c):
                p = c % 2
                act.wait_ge(s("sscan"), c + 1)
                a.activation(LS[p][:, :], Sx[p][:, 0:CH], ACT.Ln).then_inc(s("lns"), 1)

            def delta(c):
                p = c % 2
                act.wait_ge(s("delta"), deltas(c))
                if c >= 2:
                    act.wait_ge(s("ascan"), c - 1)
                    act.wait_ge(s("q"), c - 1)
                a.activation(AB[p][:, 1, :], LS[p][:, :], ACT.Exp, scale=-1.0)
                act.wait_ge(s("abin"), c + 1)
                a.activation(AB[p][:, 0, :], AB[p][:, 0, :], ACT.Exp).then_inc(s("abexp"), 1)
                a.activation(TH[p][:, :], LS[p][:, :], ACT.Tanh, scale=0.5, bias=nuh[:, 0:1]).then_inc(s("th"), 1)

            def vmm(c):
                p = c % 2
                act.wait_ge(s("vmm"), c + 1)
                if c >= 2:
                    act.wait_ge(s("y"), c - 1)
                a.activation(V[p][:, :], ps_vr[:, :], ACT.Copy).then_inc(s("v_sb"), 1)
                act.wait_ge(s("rmm"), c + 1)
                if c >= 2:
                    act.wait_ge(s("ry"), c - 1)
                a.activation(THR[p][:, :], ps_vr[:, :], ACT.Tanh, scale=0.5).then_inc(s("thr"), 1)

            def x1s(c):
                p = c % 2
                if c >= 2:
                    act.wait_ge(s("ck"), c - 1)
                before_chunk(c, h2T, s("h2T"), s("crmm"), 1, s("h20"))
                act.wait_ge(s("x2nT"), c + 1)
                a.activation(h2T[p][:, 1:CH + 1], ps_ta[:, :], ACT.Identity, scale=vcol[:, G2:G2 + 1],
                             bias=vcol[:, B2:B2 + 1]).then_inc(s("h2T"), 1)
                act.wait_ge(s("h2T"), c + 1)
                act.wait_ge(s("h20"), c + 1)
                if c >= 2:
                    act.wait_ge(s("hmm"), FB * (c - 1))
                a.activation(cx[p][:, :], h2T[p][:, 0:CH], ACT.Copy,
                             scale=omix[:, 3:4]).then_inc(s("cx"), 1)

            def ck(c):
                for i in range(FB // 2):
                    n = FB // 2 * c + i
                    act.wait_ge(s("hmm"), FB * c + 2 * i + 1)
                    if n >= 1:
                        act.wait_ge(s("kkd"), n)
                    a.activation(rl[0][:, :], ps_h[0][:, :], ACT.Relu).then_inc(s("relu0"), 1)
                    act.wait_ge(s("hmm"), FB * c + 2 * i + 2)
                    if n >= 1:
                        act.wait_ge(s("kka"), n)
                    a.activation(rl[1][:, :], ps_h[1][:, :], ACT.Relu).then_inc(s("relu1"), 1)
                    if i == 0 and c >= 2:
                        act.wait_ge(s("cvmm"), c - 1)
                    act.wait_ge(s("relu1"), n + 1)
                    a.activation(kk[c % 2][:, 2 * i + 1, :], rl[1][:, :], ACT.Square).then_inc(s("kka"), 1)

            def cr(c):
                act.wait_ge(s("crmm"), c + 1)
                if c >= 2:
                    act.wait_ge(s("p2"), c - 1)
                a.activation(thc[c % 2][:, :, :].rearrange("p j c -> p (j c)"), ps_cr[:, :], ACT.Tanh,
                             scale=0.5).then_inc(s("thc"), 1)

            def outs(c):
                act.wait_ge(s("x3T_mm"), c + 1)
                if c >= 1:
                    act.wait_ge(s("lgmm"), c)
                a.activation(x3T[:, :], ps_tb[:, :], ACT.Copy).then_inc(s("x3T"), 1)

            def route(c):
                act.wait_ge(s("r1"), c + 1)
                a.activation(ex[:, :, :], lg[:, :, :], ACT.Exp).then_inc(s("rexp"), 1)

            run({"ln1": ln1, "m": mscan, "s": sscan, "vmm": vmm, "d": delta, "x1": x1s, "ck": ck, "cr": cr,
                 "n3": outs, "r1": route})

            for e in range(E):
                p = e % 2
                act.wait_ge(s("e_T"), e + 1)
                if e >= 2:
                    act.wait_ge(s("e_h"), FB * (e - 1))
                a.activation(eT[p][:, :], [ps_ta, ps_tb][p][:, :], ACT.Copy).then_inc(s("e_x"), 1)
                if e >= 2:
                    act.wait_ge(s("e_y"), e - 1)
                for f in range(FB):
                    act.wait_ge(s("e_h"), FB * e + f + 1)
                    a.activation(kk[p][:, f, :], ps_e[f][:, :], ACT.Gelu_apprx_tanh,
                                 bias=vcol[:, NVEC + e * FB + f:NVEC + e * FB + f + 1]).then_inc(s("e_g"), 1)

        @block.vector
        def _(dve):
            v = nc.vector
            v.memset(zero[:, :], 0.0).then_inc(s("zset"), 1)
            v.memset(ohs[:, 0, :], 0.0).then_inc(s("ohs"), 1)
            def stats(c, src, mv, s_st, s_mv):
                for j in range(TPC):
                    last = v.bn_stats(st[c % 2][:, j, :], src(j))
                last.then_inc(s_st, 1)
                dve.wait_ge(s_st, c + 1)
                for j in range(TPC):
                    last = v.bn_aggr(mv[:, j, :], st[c % 2][:, j, :])
                last.then_inc(s_mv, 1)

            def vectors():
                dve.wait_ge(s("vt"), 1)
                v.tensor_copy(vcol[:, :], ps_k[:, 0:NVEC + E * FB]).then_inc(s("vcol"), 1)
                dve.wait_ge(s("vcol"), 1)
                v.tensor_scalar(omix[:, :], vcol[:, MK:MK + 5], -1.0, 1.0, ALU.mult, ALU.add).then_inc(s("wmix"), 1)
                v.tensor_scalar(nuh[:, :], vcol[:, U_:U_ + 1], -0.5, None, ALU.mult).then_inc(s("wmix"), 1)
                dve.wait_ge(s("wmix"), 2)
                dve.wait_ge(s("w_in"), W_ATT)
                for r, m in enumerate((0, 1, 2, 4)):
                    v.tensor_scalar(wm_sb[:, r, 0, :], wt_sb[:, r, :], vcol[:, MK + m:MK + m + 1], None, ALU.mult)\
                        .then_inc(s("wmix"), 1)
                    v.tensor_scalar(wm_sb[:, r, 1, :], wt_sb[:, r, :], omix[:, m:m + 1], None, ALU.mult)\
                        .then_inc(s("wmix"), 1)

            def ln1(c):
                dve.wait_ge(x_in[c], 16)
                if c >= 2:
                    dve.wait_ge(s("xn"), c - 1)
                stats(c, lambda j: x_sb[:, c, j, :], mv1[c % 2], s("ln1_st"), s("ln1_mv"))
                if c == 0:
                    vectors()

            def carry(c, buf, init, done):
                if c % CPB == 0:
                    v.memset(buf[c % 2][:, 0:1], init).then_inc(done, 1)
                else:
                    v.tensor_copy(buf[c % 2][:, 0:1], buf[1 - c % 2][:, CH:CH + 1]).then_inc(done, 1)
                dve.wait_ge(done, c + 1)

            def mscan(c):
                p = c % 2
                carry(c, Mx, NEG_INF, s("m0"))
                dve.wait_ge(s("kmm"), c + 1)
                v.tensor_tensor_scan(Mx[p][:, 1:CH + 1], vcol[:, W_:W_ + 1].broadcast_to([P, CH]), ps_k[:, :],
                                     Mx[p][:, 0:1], ALU.add, ALU.max).then_inc(s("mscan"), 1)
                dve.wait_ge(s("mscan"), c + 1)
                v.scalar_tensor_tensor(G[p][:, :], Mx[p][:, 0:CH], vcol[:, W_:W_ + 1], ps_k[:, :],
                                       ALU.add, ALU.subtract).then_inc(s("gdone"), 1)
                dve.wait_ge(s("gdone"), c + 1)
                v.tensor_scalar(EF[p][:, 0, :], G[p][:, :], 0.0, None, ALU.min)
                v.tensor_scalar(EF[p][:, 1, :], G[p][:, :], 0.0, None, ALU.max).then_inc(s("efin"), 1)

            def sscan(c):
                p = c % 2
                carry(c, Sx, 1.0, s("s0"))
                dve.wait_ge(s("efexp"), c + 1)
                v.tensor_tensor_scan(Sx[p][:, 1:CH + 1], EF[p][:, 0, :], EF[p][:, 1, :], Sx[p][:, 0:1],
                                     ALU.mult, ALU.add).then_inc(s("sscan"), 1)

            def delta(c):
                p = c % 2
                dve.wait_ge(s("lns"), c + 1)
                v.tensor_tensor(LS[p][:, :], LS[p][:, :], G[p][:, :], ALU.add).then_inc(s("delta"), 1)
                dve.wait_ge(s("delta"), deltas(c) - (c % CPB == 0))
                if c % CPB == 0:
                    v.memset(LS[p][:, 0:1], -80.0).then_inc(s("delta"), 1)
                    dve.wait_ge(s("delta"), deltas(c))
                v.tensor_scalar(AB[p][:, 0, :], LS[p][:, :], 0.0, None, ALU.min).then_inc(s("abin"), 1)

            def ys(c):
                p = c % 2
                carry(c, Ax, 0.0, s("a0"))
                dve.wait_ge(s("abexp"), c + 1)
                dve.wait_ge(s("v_sb"), c + 1)
                v.scalar_tensor_tensor(AB[p][:, 1, :], AB[p][:, 1, :], 1.0, V[p][:, :], ALU.min, ALU.mult)\
                    .then_inc(s("bv"), 1)
                dve.wait_ge(s("bv"), c + 1)
                v.tensor_tensor_scan(Ax[p][:, 1:CH + 1], AB[p][:, 0, :], AB[p][:, 1, :], Ax[p][:, 0:1],
                                     ALU.mult, ALU.add).then_inc(s("ascan"), 1)

            def y2(c):
                p = c % 2
                dve.wait_ge(s("ascan"), c + 1)
                if c >= 2:
                    dve.wait_ge(s("ryT"), c - 1)
                v.tensor_tensor(Y[p][:, :], Ax[p][:, 0:CH], V[p][:, :], ALU.subtract).then_inc(s("df"), 1)
                dve.wait_ge(s("df"), c + 1)
                dve.wait_ge(s("th"), c + 1)
                if c % CPB == 0:
                    v.memset(TH[p][:, 0:1], -1.0).then_inc(s("th0"), 1)
                    dve.wait_ge(s("th0"), c // CPB + 1)
                v.scalar_tensor_tensor(Y[p][:, :], TH[p][:, :], 1.0, Y[p][:, :], ALU.add, ALU.mult)\
                    .then_inc(s("q"), 1)
                dve.wait_ge(s("q"), c + 1)
                v.scalar_tensor_tensor(Y[p][:, :], Y[p][:, :], 0.5, V[p][:, :], ALU.mult, ALU.add)\
                    .then_inc(s("y"), 1)
                dve.wait_ge(s("y"), c + 1)
                dve.wait_ge(s("thr"), c + 1)
                v.scalar_tensor_tensor(Y[p][:, :], THR[p][:, :], 1.0, Y[p][:, :], ALU.add, ALU.mult)\
                    .then_inc(s("ry"), 1)

            def x1s(c):
                p = c % 2
                dve.wait_ge(s("ryT"), c + 1)
                if c >= 2:
                    dve.wait_ge(s("xx"), c - 1)
                v.scalar_tensor_tensor(x1[p][:, :, :].rearrange("p j c -> p (j c)"), ps_tb[:, :], 0.5,
                                       x_sb[:, c].rearrange("p j c -> p (j c)"), ALU.mult, ALU.add)\
                    .then_inc(s("x1"), 1)
                dve.wait_ge(s("x1"), c + 1)
                if c >= 2:
                    dve.wait_ge(s("x2n"), c - 1)
                stats(c, lambda j: x1[p][:, j, :], mv2[p], s("ln2_st"), s("ln2_mv"))

            def ck(c):
                p = c % 2
                dve.wait_ge(s("cx"), c + 1)
                v.scalar_tensor_tensor(cx[p][:, :], h2T[p][:, 1:CH + 1], vcol[:, CK:CK + 1], cx[p][:, :],
                                       ALU.mult, ALU.add).then_inc(s("ck"), 1)
                if c >= 2:
                    dve.wait_ge(s("cvmm"), c - 1)
                for i in range(FB // 2):
                    dve.wait_ge(s("relu0"), FB // 2 * c + i + 1)
                    v.tensor_tensor(kk[p][:, 2 * i, :], ps_h[0][:, :], rl[0][:, :], ALU.mult)\
                        .then_inc(s("kkd"), 1)

            def outs(c):
                p = c % 2
                dve.wait_ge(s("cvmm"), c + 1)
                dve.wait_ge(s("thc"), c + 1)
                if c >= 2:
                    dve.wait_ge(s("x3"), c - 1)
                zf = z[p][:, :, :].rearrange("p j c -> p (j c)")
                v.scalar_tensor_tensor(zf, thc[p][:, :, :].rearrange("p j c -> p (j c)"), 1.0, ps_cv[:, :],
                                       ALU.add, ALU.mult).then_inc(s("p2"), 1)
                dve.wait_ge(s("p2"), c + 1)
                dve.wait_ge(s("xx"), c + 1)
                v.scalar_tensor_tensor(zf, zf, 0.5, x_sb[:, c].rearrange("p j c -> p (j c)"),
                                       ALU.mult, ALU.add).then_inc(s("zz"), 1)
                dve.wait_ge(s("zz"), c + 1)
                stats(c, lambda j: z[p][:, j, :], mv3[:, c], s("ln3_st"), s("ln3_mv"))

            def n3(c):
                p = c % 2
                dve.wait_ge(s("rst3"), c + 1)
                for j in range(TPC):
                    last = v.tensor_scalar(rows[:, c, j, 0:C], z[p][:, j, :], mv3[:, c, j, 0:1],
                                           rs3[:, c, j:j + 1], ALU.subtract, ALU.mult)
                last.then_inc(s("x3"), 1)

            def wide(t):
                return t.unsqueeze(2).broadcast_to([P, TPC, E])

            def r1(c):
                p = c % 2
                lps = ps_cr[:, 0:TPC * E].rearrange("p (j e) -> p j e", e=E)
                dve.wait_ge(s("lgmm"), c + 1)
                v.tensor_reduce(mx[:, :], lps, AX.X, ALU.max).then_inc(s("r0"), 1)
                dve.wait_ge(s("r0"), c + 1)
                v.tensor_tensor(lg[:, :, :], lps, wide(mx[:, :]), ALU.subtract).then_inc(s("r1"), 1)
                dve.wait_ge(s("r1"), c + 1)
                v.scalar_tensor_tensor(cand[:, :, :], lg[:, :, :], 0.0, iota_m[:, :, :], ALU.is_equal, ALU.mult)\
                    .then_inc(s("rcand"), 1)
                dve.wait_ge(s("rcand"), c + 1)
                v.tensor_reduce(eidx[:, :], cand[:, :, :], AX.X, ALU.min).then_inc(s("ridx"), 1)
                dve.wait_ge(s("ridx"), c + 1)
                v.tensor_tensor(oh[:, :, :], iota_m[:, :, :], wide(eidx[:, :]), ALU.is_equal).then_inc(s("oh"), 1)

            def r2(c):
                p = c % 2
                rps = ps_cr[:, TPC * E:2 * TPC * E].rearrange("p (j e) -> p j e", e=E)
                dve.wait_ge(s("rexp"), c + 1)
                v.tensor_reduce(sm[:, :], ex[:, :, :], AX.X, ALU.add).then_inc(s("rsum"), 1)
                dve.wait_ge(s("rankmm"), c + 1)
                v.tensor_tensor(loc8[:, :, :], rps, oh[:, :, :], ALU.mult).then_inc(s("rloc8"), 1)
                dve.wait_ge(s("rsum"), c + 1)
                v.reciprocal(rows[:, c, :, GATE], sm[:, :]).then_inc(s("rgate"), 1)
                dve.wait_ge(s("rloc8"), c + 1)
                v.tensor_reduce(loc[:, :], loc8[:, :, :], AX.X, ALU.add).then_inc(s("rloc"), 1)
                v.tensor_reduce(ohr[:, :], oh[:, :, :].rearrange("p j e -> p e j"), AX.X, ALU.add)\
                    .then_inc(s("rsub"), 1)
                dve.wait_ge(s("rloc"), c + 1)
                v.scalar_tensor_tensor(slot[:, :], eidx[:, :], float(CAP), loc[:, :], ALU.mult, ALU.add)
                v.tensor_scalar(pen[:, :], loc[:, :], float(CAP), float(4 * N), ALU.is_ge, ALU.mult)\
                    .then_inc(s("rslot"), 1)
                dve.wait_ge(s("rsub"), c + 1)
                v.tensor_tensor(ohs[:, 1 - p, :], ohs[:, p, :], ohr[:, :], ALU.add).then_inc(s("ohs"), 1)
                dve.wait_ge(s("rslot"), c + 1)
                if c >= 2:
                    dve.wait_ge(scat[c - 2], 16 * TPC)
                v.scalar_tensor_tensor(sidx[p][:, :], slot[:, :], float(E * CAP), pen[:, :], ALU.add, ALU.add)\
                    .then_inc(s("sidx"), 1)

            run({"ln1": ln1, "m": mscan, "s": sscan, "d": delta, "y1": ys, "y2": y2, "x1": x1s, "ck": ck,
                 "z": outs, "n3": n3, "r1": r1, "r2": r2})

            def finish(e):
                p = e % 2
                dve.wait_ge(s("e_rst"), e + 1)
                if e >= NEO:
                    dve.wait_ge(osc[e % NEO], 16 * SPE * (e // NEO))
                for j in range(SPE):
                    last = v.tensor_scalar(eo[e % NEO][:, j, :], z[p][:, j, :], mv1[p][:, j, 0:1],
                                           rs[:, 0, p, j:j + 1], ALU.subtract, ALU.mult)
                last.then_inc(s("e_norm"), 1)

            dve.wait_ge(s("we_in"), W_EXP)
            for e in range(E):
                p = e % 2
                dve.wait_ge(e_in[e], 16)
                v.tensor_copy(tid[:, e, :], er[:, e, :, TOK]).then_inc(s("e_tid"), 1)
                dve.wait_ge(s("e_y"), e + 1)
                if e >= 2:
                    dve.wait_ge(s("e_norm"), e - 1)
                yb = [ps_cv, ps_cr][p][:, :].rearrange("p (j c) -> p j c", c=C)
                v.tensor_tensor(z[p][:, :, :], yb, b2_sb[:, e:e + 1, :].broadcast_to([P, SPE, C]), ALU.add)\
                    .then_inc(s("e_yb"), 1)
                dve.wait_ge(s("e_yb"), e + 1)
                for j in range(SPE):
                    last = v.scalar_tensor_tensor(z[p][:, j, :], z[p][:, j, :], er[:, e, j, GATE:GATE + 1],
                                                  er[:, e, j, 0:C], ALU.mult, ALU.add)
                last.then_inc(s("e_z"), 1)
                dve.wait_ge(s("e_z"), e + 1)
                stats(e, lambda j: z[p][:, j, :], mv1[p], s("e_st"), s("e_mv"))
                if e >= 1:
                    finish(e - 1)
            finish(E - 1)

        @block.tensor
        def _(pe):
            t_ = nc.tensor
            NV = NVEC + E * FB
            pe.wait_ge(s("cst"), 6)
            pe.wait_ge(s("v_in"), 16 * 12)
            t_.transpose(ps_k[:, 0:NV], vrows[:, :], ident[0:NV, 0:NV]).then_inc(s("vt"), 1)

            def turn(dst, src, done):
                for j in range(TPC):
                    last = t_.transpose(dst[:, j * TILE:(j + 1) * TILE], src(j), ident[:, :])
                last.then_inc(done, 1)

            def mixed(dst, r, c, done):
                t_.matmul(dst[:, :], wm_sb[:, r, 0, :], hT[c % 2][:, 1:CH + 1], start=True, stop=False)
                t_.matmul(dst[:, :], wm_sb[:, r, 1, :], hT[c % 2][:, 0:CH], start=False, stop=True)\
                    .then_inc(done, 1)

            ta_users = (("ln1", s("hT")), ("x1", s("h2T")))
            tb_users = (("y2", s("x1")), ("n3", s("x3T")))

            def ln1(c):
                pe.wait_ge(s("xn"), c + 1)
                freed(pe, "ln1", c, *ta_users)
                turn(ps_ta, lambda j: xn[c % 2][:, j, :], s("xnT"))

            def kmm(c):
                if c == 0:
                    pe.wait_ge(s("wmix"), 10)
                pe.wait_ge(s("hT"), c + 1)
                pe.wait_ge(s("h0"), c + 1)
                if c >= 1:
                    pe.wait_ge(s("gdone"), c)
                mixed(ps_k, 0, c, s("kmm"))

            def vmm(c):
                if c >= 1:
                    pe.wait_ge(s("thr"), c)
                mixed(ps_vr, 1, c, s("vmm"))
                pe.wait_ge(s("v_sb"), c + 1)
                mixed(ps_vr, 2, c, s("rmm"))

            def y2(c):
                pe.wait_ge(s("ry"), c + 1)
                freed(pe, "y2", c, *tb_users)
                turn(ps_tb, lambda j: Y[c % 2][:, j * TILE:(j + 1) * TILE], s("ryT"))

            def x1s(c):
                pe.wait_ge(s("x2n"), c + 1)
                freed(pe, "x1", c, *ta_users)
                turn(ps_ta, lambda j: x2n[c % 2][:, j, :], s("x2nT"))

            def ck(c):
                pe.wait_ge(s("ck"), c + 1)
                for f in range(FB):
                    n = FB // 2 * c + f // 2
                    if n >= 1:
                        pe.wait_ge(s("relu1") if f % 2 else s("kkd"), n)
                    t_.matmul(ps_h[f % 2][:, :], wck_sb[:, f * P:(f + 1) * P], cx[c % 2][:, :], start=True, stop=True)\
                        .then_inc(s("hmm"), 1)

            def cr(c):
                pe.wait_ge(s("h2T"), c + 1)
                pe.wait_ge(s("h20"), c + 1)
                if c == 0:
                    pe.wait_ge(s("wmix"), 10)
                freed(pe, "cr", c, ("n3", s("rloc8")))
                for j in range(TPC):
                    o = ps_cr[:, j * C:(j + 1) * C]
                    h2 = h2T[c % 2]
                    t_.matmul(o, h2[:, 1 + j * TILE:1 + (j + 1) * TILE], wm_sb[:, 3, 0, :], start=True, stop=False)
                    last = t_.matmul(o, h2[:, j * TILE:(j + 1) * TILE], wm_sb[:, 3, 1, :], start=False, stop=True)
                last.then_inc(s("crmm"), 1)

            def cv(c):
                p = c % 2
                pe.wait_ge(s("kkd"), FB // 2 * (c + 1))
                pe.wait_ge(s("kka"), FB // 2 * (c + 1))
                if c >= 1:
                    pe.wait_ge(s("p2"), c)
                for j in range(TPC):
                    for f in range(FB):
                        last = t_.matmul(ps_cv[:, j * C:(j + 1) * C], kk[p][:, f, j * TILE:(j + 1) * TILE],
                                         wcv_sb[:, f, :], start=(f == 0), stop=(f == FB - 1))
                last.then_inc(s("cvmm"), 1)

            def n3(c):
                pe.wait_ge(s("x3"), c + 1)
                freed(pe, "n3", c, *tb_users)
                turn(ps_tb, lambda j: rows[:, c, j, 0:C], s("x3T_mm"))
                pe.wait_ge(s("x3T"), c + 1)
                freed(pe, "n3", c, ("cr", s("thc")), ("n3", s("rloc8")))
                for j in range(TPC):
                    last = t_.matmul(ps_cr[:, j * E:(j + 1) * E], x3T[:, j * TILE:(j + 1) * TILE], wg_sb[:, :],
                                     start=True, stop=True)
                last.then_inc(s("lgmm"), 1)

            def r1(c):
                R = TPC * E
                pe.wait_ge(s("oh"), c + 1)
                pe.wait_ge(s("ohs"), c + 1)
                ohf = oh[:, :, :].rearrange("p j e -> p (j e)")
                t_.matmul(ps_cr[:, R:2 * R], tri[:, :], ohf, start=True, stop=False)
                t_.matmul(ps_cr[:, R:2 * R].rearrange("p (j e) -> p j e", e=E), ones[:, :],
                          ohs[:, c % 2:c % 2 + 1, :].broadcast_to([P, TPC, E]), start=False, stop=False)
                for i in range(TPC - 1):
                    last = t_.matmul(ps_cr[:, R + (i + 1) * E:2 * R].rearrange("p (j e) -> p j e", e=E), ones[:, :],
                                     oh[:, i:i + 1, :].broadcast_to([P, TPC - 1 - i, E]),
                                     start=False, stop=(i == TPC - 2))
                last.then_inc(s("rankmm"), 1)

            run({"ln1": ln1, "kmm": kmm, "vmm": vmm, "y2": y2, "x1": x1s, "ck": ck, "cr": cr, "cv": cv,
                 "n3": n3, "r1": r1})

            pe.wait_ge(s("we_in"), W_EXP)

            def second(e):
                p = e % 2
                pe.wait_ge(s("e_g"), FB * (e + 1))
                if e >= 2:
                    pe.wait_ge(s("e_yb"), e - 1)
                if e == 1:
                    pe.wait_ge(s("rloc8"), NCH)
                for j in range(SPE):
                    for f in range(FB):
                        last = t_.matmul([ps_cv, ps_cr][p][:, j * C:(j + 1) * C], kk[p][:, f, j * TILE:(j + 1) * TILE],
                                         w2_sb[:, e, f, :], start=(f == 0), stop=(f == FB - 1))
                last.then_inc(s("e_y"), 1)

            def expand(e):
                p = e % 2
                pe.wait_ge(e_in[e], 16)
                if e >= 2:
                    pe.wait_ge(s("e_x"), e - 1)
                turn([ps_ta, ps_tb][p], lambda j: er[:, e, j, 0:C], s("e_T"))

            expand(0)
            for e in range(E):
                p = e % 2
                pe.wait_ge(s("e_x"), e + 1)
                for f in range(FB):
                    n = FB * e + f
                    if n >= 4:
                        pe.wait_ge(s("e_g"), n - 3)
                    t_.matmul(ps_e[f][:, :], w1_sb[:, e, f * P:(f + 1) * P], eT[p][:, :], start=True, stop=True)\
                        .then_inc(s("e_h"), 1)
                if e + 1 < E:
                    expand(e + 1)
                if e >= 1:
                    second(e - 1)
            second(E - 1)


_INS = ['L0_attn_x', 'L0_attn_time_decay', 'L0_attn_time_first', 'L0_attn_w_tk', 'L0_attn_w_tv', 'L0_attn_w_tr',
        'L0_attn_w_ck', 'L0_attn_w_cv', 'L0_attn_w_cr', 'L0_attn_ln1_g', 'L0_attn_ln1_b', 'L0_attn_ln2_g',
        'L0_attn_ln2_b', 'L0_attn_mix_k', 'L0_attn_mix_v', 'L0_attn_mix_r', 'L0_attn_cmix_k', 'L0_attn_cmix_r',
        'L0_ffn_wg', 'L0_ffn_w1', 'L0_ffn_b1', 'L0_ffn_w2', 'L0_ffn_b2']
_OUTS = [((2, 2048, 128), 'float32')]


def kernel(**inputs):
    import numpy as _np
    import concourse.bacc as _bacc
    from concourse import mybir as _mybir
    from concourse.bass_utils import run_bass_kernel_spmd as _run

    nc = _bacc.Bacc("TRN2", target_bir_lowering=False, num_devices=1)
    arrays, args = {}, []
    for name in _INS:
        a = _np.ascontiguousarray(inputs[name])
        arrays[f"in_{name}_dram"] = a
        args.append(nc.dram_tensor(f"in_{name}_dram", a.shape, _mybir.dt.from_np(a.dtype), kind="ExternalInput").ap())
    for i, (shape, dtype) in enumerate(_OUTS):
        dt = _mybir.dt.from_np(_np.dtype(dtype))
        args.append(nc.dram_tensor(f"out_{i}_dram", shape, dt, kind="ExternalOutput").ap())
    rwkv_moe_kernel(nc, *args)
    r = _run(nc, [arrays], core_ids=[0])
    return r.results[0]["out_0_dram"]
```

```python
from contextlib import ExitStack

import concourse.bass as bass
from concourse import mybir

ALU = mybir.AluOpType
ACT = mybir.ActivationFunctionType
AX = mybir.AxisListType
F32 = mybir.dt.float32
F32R = mybir.dt.float32r
BF16 = mybir.dt.bfloat16
U32 = mybir.dt.uint32

P = 128
LN_EPS = 1e-05
NEG_INF = -1e38
BIG = 3e38
W_, U_, G1, B1, G2, B2, MK, MV, MR, CK, CR = range(11)
NVEC = 11


def rwkv_moe_kernel(nc, x, time_decay, time_first, w_tk, w_tv, w_tr, w_ck, w_cv, w_cr,
                    ln1_g, ln1_b, ln2_g, ln2_b, mix_k, mix_v, mix_r, cmix_k, cmix_r,
                    wg, w1, b1, w2, b2, out):
    B, T, C = x.shape
    E, _, F = w1.shape
    N = B * T
    TILE = P
    CH = 512
    TPC = CH // TILE
    NT = N // TILE
    CHUNKS = [[TPC] * (T // CH)] * B
    assert T % CH == 0
    nt = [n for row in CHUNKS for n in row]
    NCH = len(nt)
    t0 = [sum(nt[:c]) for c in range(NCH)]
    ntok = [n * TILE for n in nt]
    row0 = [t * TILE % T == 0 for t in t0]
    FB = F // P
    CAP = (N + E - 1) // E
    SPE = CAP // TILE
    ROW = C + 2
    GATE, TOK = C, C + 1
    assert C == P and CAP == CH and F == 4 * P

    xf = x.rearrange("b (t p) c -> p (b t) c", p=TILE)
    of = out.rearrange("b (t p) c -> p (b t) c", p=TILE)
    out_rows = out.rearrange("b t c -> (b t) c")
    disp = nc.dram_tensor("disp", [E * CAP, ROW], F32, kind="Internal").ap()
    disp_t = disp[:, :].rearrange("(e j p) r -> e p j r", p=TILE, j=SPE)

    with ExitStack() as ctx:
        def sb(name, shape, dt=F32):
            return ctx.enter_context(nc.sbuf_tensor(name, shape, dt))

        def sem(name):
            return ctx.enter_context(nc.semaphore(name))

        def bank(name):
            return ctx.enter_context(nc.psum_tensor(name, [P, 512], F32))

        ps_k, ps_vr, ps_ta, ps_tb = bank("ps_k"), bank("ps_vr"), bank("ps_ta"), bank("ps_tb")
        ps_h = [bank("ps_h0"), bank("ps_h1")]
        ps_cv, ps_cr = bank("ps_cv"), bank("ps_cr")
        ps_e = [ps_h[0], ps_h[1], ps_k, ps_vr]

        x_raw = sb("x_raw", [P, E * SPE * ROW])
        x_sb = x_raw[:, 0:N // P * C].rearrange("p (t c) -> p t c", c=C)
        er = x_raw[:, :].rearrange("p (e j r) -> p e j r", j=SPE, r=ROW)
        vrows = sb("vrows", [NVEC + E * FB, P])
        vcol = sb("vcol", [P, NVEC + E * FB])
        wt_sb = sb("wt_sb", [P, 4, C])
        wm_sb = sb("wm_sb", [P, 4, 2, C])
        wck_sb = sb("wck_sb", [P, F])
        wcv_sb = sb("wcv_sb", [P, FB, C])
        wg_sb = sb("wg_sb", [P, E])
        w2_sb = sb("w2_sb", [P, E, FB, C])
        ident = sb("ident", [P, P])
        tri = sb("tri", [P, P], BF16)
        ones = sb("ones", [P, P], BF16)
        mhalf = sb("mhalf", [P, NT])
        iota_m = sb("iota_m", [P, TPC, E])
        omix = sb("omix", [P, 5])
        nuh = sb("nuh", [P, 1])
        fill = sb("fill", [P, SPE, ROW])
        rows = sb("rows", [P, NT, ROW])
        mv3 = sb("mv3", [P, NT, 2])
        rs3 = sb("rs3", [P, NT])
        zero = sb("zero", [P, 1])
        def two(name, shape, dt=F32):
            return [sb(f"{name}{i}", shape, dt) for i in range(2)]

        hT, h2T = two("hT", [P, CH + 1]), two("h2T", [P, CH + 1])
        mv1, mv2 = two("mv1", [P, TPC, 2]), two("mv2", [P, TPC, 2])
        st = [two(f"st{k}_", [P, TPC, 6]) for k in range(3)]
        lnw = sb("lnw", [P, 3, 2, TPC])
        nmr = sb("nmr", [P, 2, 2, 2, TPC])
        rs = sb("rs", [P, 2, 2, TPC])
        xn = two("xn", [P, TPC, C])
        Mx = two("Mx", [P, CH + 1])
        Sx = two("Sx", [P, CH + 1])
        Ax = two("Ax", [P, CH + 1])
        G = two("G", [P, CH])
        EF = two("EF", [P, 2, CH])
        LS = two("LS", [P, CH])
        AB = two("AB", [P, 2, CH])
        V = two("V", [P, CH])
        TH = two("TH", [P, CH])
        THR = two("THR", [P, CH])
        Y = two("Y", [P, CH])
        x1 = two("x1", [P, TPC, C])
        x2n = two("x2n", [P, TPC, C])
        cx = two("cx", [P, CH])
        kk = two("kk", [P, FB, CH])
        thc = two("thc", [P, CH])
        z = two("z", [P, CH])
        dsc = sb("dsc", [P, 3, NT])
        x3T = sb("x3T", [P, CH])
        mx = sb("mx", [P, TPC])
        lg = sb("lg", [P, TPC, E])
        ex = sb("ex", [P, TPC, E])
        sm = sb("sm", [P, TPC])
        cand = sb("cand", [P, TPC, E])
        eidx = sb("eidx", [P, TPC])
        oh = sb("oh", [P, TPC, E], BF16)
        ohs = sb("ohs", [P, 2, E], BF16)
        ohr = sb("ohr", [P, E])
        loc8 = sb("loc8", [P, TPC, E])
        loc = sb("loc", [P, TPC])
        pen = sb("pen", [P, TPC])
        slot = sb("slot", [P, TPC])
        sidx = two("sidx", [P, TPC], U32)
        xhi = [t[:, :] for t in two("xhi", [P, CAP], F32R)]
        xlo = [t[:, :] for t in two("xlo", [P, CAP], F32R)]
        w1hi_sb, w1lo_sb = sb("w1hi_sb", [P, E, F], F32R), sb("w1lo_sb", [P, E, F], F32R)
        w1raw = [[EF[0], EF[1], AB[0], AB[1]][e // 2][:, e % 2, :] for e in range(E)]
        b2_sb = [G[e // (CH // C)][:, e % (CH // C) * C:(e % (CH // C) + 1) * C] for e in range(E)]
        tid = sb("tid", [P, E, SPE], U32)
        eo = [xn[0], xn[1], x2n[0], x2n[1]]
        NEO = 4
        UNITS = [(e, 0, SPE) for e in range(E - 1)] + [(E - 1, 0, SPE // 2), (E - 1, SPE // 2, SPE // 2)]
        NU = len(UNITS)

        def sent(u):
            return sum(UNITS[k][2] for k in range(u % NEO, u, NEO))


        S = {}

        def s(name):
            if name not in S:
                S[name] = sem(name)
            return S[name]

        names = """th0 h0 h20 rst3 kka wc_in b2_in dsc e_rst w_in we_in v_in vt vcol cst id0 fillset disp_fill
            wmix zset ln1_st ln1_mv ln_pool xn xnT hT kmm vmm rmm m0 mscan gdone efin efexp s0 sscan lns delta
            abin abexp th v_sb thr bv a0 ascan df q y ry ryT x1 ln2_st ln2_mv x2n x2nT h2T cx ck hmm relu crmm
            thc cvmm p2 zz ln3_st ln3_mv xx x3 drop x3T_mm x3T lgmm r0 r1 rexp rsum rgate rcand ridx oh rankmm
            ohs rloc8 rloc rslot rsub sidx e_T e_x e_xlo e_w1hi e_w1lo e_h e_g e_y e_yb e_z e_st e_mv e_norm
            e_tid""".split()
        for n_ in names:
            s(n_)
        x_in = [sem(f"x_in{c}") for c in range(NCH)]
        e_in = [sem(f"e_in{e}") for e in range(E)]
        w1_in = [sem(f"w1_in{e}") for e in range(E)]
        scat = [sem(f"scat{c}") for c in range(NCH)]
        osc = [sem(f"osc{i}") for i in range(NEO)]
        dout = sem("dout")

        START = [0.00, 0.89, 1.82, 2.92, 3.96, 5.03, 6.16, 7.31]
        STRETCH = [0.856, 0.890, 0.929, 0.941, 0.968, 0.997, 1.019, 1.041]
        AT = dict(
            dve=dict(ln1=-0.009, ln1m=0.106, m1=1.382, m2=1.413, m3=1.461, s=1.902, d1=2.198, d2=2.465, bv=2.692,
                     aa=2.947, df=3.086, yq=3.303, yy=3.308, ry=3.313, x1=3.473, x1s=3.511, x1m=3.579, ck=4.074,
                     p2=5.141, zz=5.182, zs=5.210, zm=5.335, x3=5.646, r0=5.995, r1=6.139, rc=6.142, ri=6.237,
                     oh=6.304, r2=6.409, r3=6.449, r4=6.653),
            pe=dict(ln1m=0.761, kmm=1.518, vmm=2.252, rmm=2.790, ry=3.560, x1m=3.949, cr=4.175, ck=4.604, kk1=4.748,
                    cv=5.113, x3=5.973, lg=6.115, oh=6.386),
            act=dict(ln1m=0.992, m3=1.991, s=2.210, vmm=2.582, d2=2.667, rmm=2.923, x1m=4.033, cr=4.406, kk1=4.683,
                     kk2=4.919, x3=6.152, r1=6.428),
            pool=dict(ln1m=1.394, x1m=4.907, xx=5.052, zm=6.292, r4=8.455))
        STAGES = list(dict.fromkeys(n for e in AT.values() for n in e))

        def when(eng, stage, c):
            return START[c] + AT[eng][stage] * STRETCH[c], STAGES.index(stage), c

        for written, last_read, buffers in (
                ("ln1", "ln1m", 2), ("x1s", "x1m", 2), ("zs", "zm", 2), ("m1", "m2", 2), ("m2", "d1", 2), ("m3", "s", 2),
                ("s", "d2", 2), ("d2", "aa", 2), ("aa", "df", 2), ("x1", "x1s", 2), ("p2", "x3", 2), ("r0", "r4", 1)):
            for c in range(buffers, NCH):
                assert when("dve", last_read, c - buffers) < when("dve", written, c)
        for eng, stages in AT.items():
            for n_ in stages:
                assert all(when(eng, n_, c - 1) < when(eng, n_, c) for c in range(1, NCH))

        def run(eng, **fns):
            assert set(fns) == set(AT[eng])
            for _, n, c in sorted(when(eng, n, c) for n in fns for c in range(NCH)):
                fns[STAGES[n]](c)

        def freed(eng, at, c, *users):
            for stage, read in users:
                n = sum(when("pe", stage, k) < when("pe", at, c) for k in range(NCH))
                if n:
                    eng.wait_ge(read, n)

        def deltas(c):
            return c + 1 + sum(row0[:c + 1])

        block = ctx.enter_context(nc.Block())

        @block.sync
        def _(sp):
            def load(c):
                t = slice(t0[c], t0[c] + nt[c])
                sp.dma_start(x_sb[:, t], xf[:, t]).then_inc(x_in[c], 16)

            load(0)
            for r, v_ in enumerate((mix_k, mix_v, mix_r, cmix_k, cmix_r)):
                sp.dma_start(vrows[6 + r:7 + r, :], v_.rearrange("a b c -> (a b) c")).then_inc(s("v_in"), 16)
            for r, w_ in enumerate((w_tk, w_tv, w_tr, w_cr)):
                sp.dma_start(wt_sb[:, r, :], w_).then_inc(s("w_in"), 16)
            load(1)
            sp.dma_start(wck_sb[:, :], w_ck).then_inc(s("wc_in"), 16)
            sp.dma_start(wcv_sb[:, :, :], w_cv.rearrange("(f p) c -> p f c", p=P)).then_inc(s("wc_in"), 16)
            sp.dma_start(wg_sb[:, :], wg).then_inc(s("wc_in"), 16)
            load(2)
            sp.wait_ge(s("fillset"), 2)
            for e in range(E):
                sp.dma_start(disp_t[e], fill[:, :, :]).then_inc(s("disp_fill"), 16)
            for c in range(3, NCH):
                load(c)
            for e in range(E):
                sp.dma_start(w2_sb[:, e, :, :], w2[e].rearrange("(f p) c -> p f c", p=P)).then_inc(s("we_in"), 16)
            sp.wait_ge(s("sscan"), NCH)
            sp.wait_ge(s("ascan"), NCH)
            sp.wait_ge(s("delta"), deltas(NCH - 1))
            for e in range(E):
                sp.dma_start(w1raw[e], w1[e]).then_inc(w1_in[e], 16)
            for e in range(E):
                sp.dma_start(b2_sb[e], b2[e].partition_broadcast(P)).then_inc(s("b2_in"), 16)
            for c in range(NCH):
                sp.wait_ge(scat[c], 16 * nt[c])
            for e in range(E):
                sp.dma_start(er[:, e], disp_t[e]).then_inc(e_in[e], 16)
            for c in range(NCH):
                sp.wait_ge(s("drop"), c + 1)
                t = slice(t0[c], t0[c] + nt[c])
                sp.dma_start(of[:, t], rows[:, t, 0:C]).then_inc(dout, 16)
            sp.wait_ge(dout, 16 * NCH)


        @block.gpsimd
        def _(pool):
            g = nc.gpsimd
            g.memset(fill[:, :, :], 0.0).then_inc(s("fillset"), 1)
            pool.wait_ge(s("fillset"), 1)
            g.memset(fill[:, :, TOK:TOK + 1], float(4 * N)).then_inc(s("fillset"), 1)
            g.memset(ident[:, :], 0.0).then_inc(s("id0"), 1)
            g.memset(tri[:, :], 1.0).then_inc(s("id0"), 1)
            g.memset(ones[:, :], 1.0).then_inc(s("cst"), 1)
            g.memset(mhalf[:, :], -0.5).then_inc(s("cst"), 1)
            pool.wait_ge(s("id0"), 2)
            g.affine_select(out=ident[:, :], in_=ident[:, :], compare_op=ALU.not_equal, fill=1.0, base=0,
                            pattern=[[-1, P]], channel_multiplier=1).then_inc(s("cst"), 1)
            g.affine_select(out=tri[:, :], in_=tri[:, :], compare_op=ALU.is_gt, fill=0.0, base=0,
                            pattern=[[1, P]], channel_multiplier=-1).then_inc(s("cst"), 1)
            g.iota(iota_m[:, :, :], pattern=[[0, TPC], [1, E]], base=-E, channel_multiplier=0,
                   allow_small_or_imprecise_dtypes=True).then_inc(s("cst"), 1)
            g.iota(rows[:, :, TOK], pattern=[[TILE, NT]], base=0, channel_multiplier=1,
                   allow_small_or_imprecise_dtypes=True).then_inc(s("cst"), 1)
            step = [0]

            def link(ins):
                step[0] += 1
                ins.then_inc(s("ln_pool"), 1)
                pool.wait_ge(s("ln_pool"), step[0])

            def rstd(w, var, dst, done=None):
                link(g.tensor_scalar(w, var, 1.0, LN_EPS, ALU.mult, ALU.add))
                last = g.tensor_tensor(dst, w, mhalf[:, 0:w.shape[1]], ALU.pow)
                if done is None:
                    link(last)
                else:
                    last.then_inc(done, 1)

            def norm(k, c, mv, src, dst, done):
                p, n = c % 2, nt[c]
                nm, r = nmr[:, k, p, 0, 0:n], rs[:, k, p, 0:n]
                g.tensor_scalar(nm, mv[:, 0:n, 0], -1.0, 0.0, ALU.mult, ALU.add)
                rstd(lnw[:, k, p, 0:n], mv[:, 0:n, 1], r)
                link(g.tensor_tensor(nmr[:, k, p, 1, 0:n], nm, r, ALU.mult))
                for j in range(n):
                    last = g.tensor_scalar(dst(j), src(j), rs[:, k, p, j:j + 1], nmr[:, k, p, 1, j:j + 1],
                                           ALU.mult, ALU.add)
                last.then_inc(done, 1)

            def ln1(c):
                p = c % 2
                if c == 0:
                    pool.wait_ge(s("cst"), 6)
                pool.wait_ge(s("ln1_mv"), c + 1)
                if c >= 2:
                    pool.wait_ge(s("xnT"), c - 1)
                norm(0, c, mv1[p], lambda j: x_sb[:, t0[c] + j, :], lambda j: xn[p][:, j, :], s("xn"))

            def norm2(c):
                p = c % 2
                pool.wait_ge(s("ln2_mv"), c + 1)
                if c >= 2:
                    pool.wait_ge(s("x2nT"), c - 1)
                norm(1, c, mv2[p], lambda j: x1[p][:, j, :], lambda j: x2n[p][:, j, :], s("x2n"))

            def xx(c):
                xc = x_sb[:, t0[c]:t0[c] + nt[c]]
                pool.wait_ge(s("x1"), c + 1)
                pool.wait_ge(s("xn"), c + 1)
                g.tensor_tensor(xc, xc, x1[c % 2][:, 0:nt[c], :], ALU.add).then_inc(s("xx"), 1)

            def rstd3(c):
                t = slice(t0[c], t0[c] + nt[c])
                pool.wait_ge(s("ln3_mv"), c + 1)
                rstd(lnw[:, 2, c % 2, 0:nt[c]], mv3[:, t, 1], rs3[:, t], s("rst3"))

            def scatter(c):
                p = c % 2
                if c == 0:
                    pool.wait_ge(s("disp_fill"), 16 * E)
                pool.wait_ge(s("rgate"), c + 1)
                pool.wait_ge(s("sidx"), c + 1)
                for j in range(nt[c]):
                    g.indirect_dma_start(out=disp[:, :], out_offset=bass.IndirectOffsetOnAxis(ap=sidx[p][:, j:j + 1], axis=0),
                                         in_=rows[:, t0[c] + j, :], in_offset=None, bounds_check=E * CAP - 1,
                                         oob_is_err=False).then_inc(scat[c], 16)

            def drop_scale():
                link(g.tensor_tensor(dsc[:, 0, :], rs3[:, :], rs3[:, :], ALU.mult))
                link(g.tensor_tensor(dsc[:, 1, :], dsc[:, 0, :], mv3[:, :, 1], ALU.mult))
                link(g.tensor_scalar(dsc[:, 0, :], dsc[:, 1, :], 1.0, LN_EPS, ALU.mult, ALU.add))
                g.tensor_tensor(dsc[:, 2, :], dsc[:, 0, :], mhalf[:, :], ALU.pow).then_inc(s("dsc"), 1)

            run("pool", ln1m=ln1, x1m=norm2, xx=xx, zm=rstd3, r4=scatter)
            pool.wait_ge(s("rst3"), NCH)
            drop_scale()

            def e_rstd(u):
                p, n = u % 2, UNITS[u][2]
                pool.wait_ge(s("e_mv"), u + 1)
                if u >= 2:
                    pool.wait_ge(s("e_norm"), u - 1)
                rstd(lnw[:, 0, p, 0:n], mv1[p][:, 0:n, 1], rs[:, 0, p, 0:n], s("e_rst"))

            def send(u):
                e, j0, n = UNITS[u]
                if u == 0:
                    pool.wait_ge(dout, 16 * NCH)
                pool.wait_ge(s("e_norm"), u + 1)
                for j in range(n):
                    g.indirect_dma_start(out=out_rows,
                                         out_offset=bass.IndirectOffsetOnAxis(ap=tid[:, e, j0 + j:j0 + j + 1], axis=0),
                                         in_=eo[u % NEO][:, j, :], in_offset=None, bounds_check=N - 1,
                                         oob_is_err=False).then_inc(osc[u % NEO], 16)

            for u in range(NU - 2):
                e_rstd(u)
                send(u)
            e_rstd(NU - 2)
            e_rstd(NU - 1)
            send(NU - 2)
            send(NU - 1)
            for i in range(NEO):
                pool.wait_ge(osc[i], 16 * sum(UNITS[k][2] for k in range(i, NU, NEO)))

        @block.scalar
        def _(act):
            a = nc.scalar
            for r, v_ in enumerate((time_decay, time_first, ln1_g, ln1_b, ln2_g, ln2_b)):
                act.dma_start(vrows[r:r + 1, :], v_.rearrange("(a c) -> a c", a=1)).then_inc(s("v_in"), 16)
            act.dma_start(vrows[NVEC:, :], b1.rearrange("e (j p) -> (e j) p", p=P)).then_inc(s("v_in"), 16)

            def before_chunk(c, buf, written, read, per, done):
                p = c % 2
                if c >= 2:
                    act.wait_ge(read, per * (c - 1))
                if row0[c]:
                    src = zero[:, 0:1]
                else:
                    src = buf[1 - p][:, ntok[c - 1]:ntok[c - 1] + 1]
                    act.wait_ge(written, c)
                a.activation(buf[p][:, 0:1], src, ACT.Copy).then_inc(done, 1)

            def ln1(c):
                p = c % 2
                if c == 0:
                    act.wait_ge(s("vcol"), 1)
                    act.wait_ge(s("zset"), 1)
                before_chunk(c, hT, s("hT"), s("rmm"), 1, s("h0"))
                act.wait_ge(s("xnT"), c + 1)
                a.activation(hT[p][:, 1:ntok[c] + 1], ps_ta[:, 0:ntok[c]], ACT.Identity, scale=vcol[:, G1:G1 + 1],
                             bias=vcol[:, B1:B1 + 1]).then_inc(s("hT"), 1)

            def mscan(c):
                p, n = c % 2, ntok[c]
                act.wait_ge(s("efin"), c + 1)
                a.activation(EF[p][:, 0, 0:n], EF[p][:, 0, 0:n], ACT.Exp)
                a.activation(EF[p][:, 1, 0:n], EF[p][:, 1, 0:n], ACT.Exp, scale=-1.0).then_inc(s("efexp"), 1)

            def sscan(c):
                p, n = c % 2, ntok[c]
                act.wait_ge(s("sscan"), c + 1)
                a.activation(LS[p][:, 0:n], Sx[p][:, 0:n], ACT.Ln).then_inc(s("lns"), 1)

            def delta(c):
                p, n = c % 2, ntok[c]
                act.wait_ge(s("delta"), deltas(c))
                if c >= 2:
                    act.wait_ge(s("ascan"), c - 1)
                    act.wait_ge(s("q"), c - 1)
                a.activation(AB[p][:, 1, 0:n], LS[p][:, 0:n], ACT.Exp, scale=-1.0)
                act.wait_ge(s("abin"), c + 1)
                a.activation(AB[p][:, 0, 0:n], AB[p][:, 0, 0:n], ACT.Exp).then_inc(s("abexp"), 1)
                a.activation(TH[p][:, 0:n], LS[p][:, 0:n], ACT.Tanh, scale=0.5, bias=nuh[:, 0:1]).then_inc(s("th"), 1)

            def v_copy(c):
                p, n = c % 2, ntok[c]
                act.wait_ge(s("vmm"), c + 1)
                if c >= 2:
                    act.wait_ge(s("y"), c - 1)
                a.activation(V[p][:, 0:n], ps_vr[:, 0:n], ACT.Copy).then_inc(s("v_sb"), 1)

            def r_tanh(c):
                p, n = c % 2, ntok[c]
                act.wait_ge(s("rmm"), c + 1)
                if c >= 2:
                    act.wait_ge(s("ry"), c - 1)
                a.activation(THR[p][:, 0:n], ps_vr[:, 0:n], ACT.Tanh, scale=0.5).then_inc(s("thr"), 1)

            def x1s(c):
                p = c % 2
                if c >= 2:
                    act.wait_ge(s("ck"), c - 1)
                before_chunk(c, h2T, s("h2T"), s("crmm"), 1, s("h20"))
                act.wait_ge(s("x2nT"), c + 1)
                a.activation(h2T[p][:, 1:ntok[c] + 1], ps_ta[:, 0:ntok[c]], ACT.Identity, scale=vcol[:, G2:G2 + 1],
                             bias=vcol[:, B2:B2 + 1]).then_inc(s("h2T"), 1)
                act.wait_ge(s("h2T"), c + 1)
                act.wait_ge(s("h20"), c + 1)
                if c >= 2:
                    act.wait_ge(s("hmm"), FB * (c - 1))
                a.activation(cx[p][:, 0:ntok[c]], h2T[p][:, 0:ntok[c]], ACT.Copy,
                             scale=omix[:, 3:4]).then_inc(s("cx"), 1)

            def relu_square(i):
                def go(c):
                    p = c % 2
                    if i == 0 and c >= 2:
                        act.wait_ge(s("cvmm"), c - 1)
                    for f in range(2 * i, 2 * i + 2):
                        act.wait_ge(s("hmm"), FB * c + f + 1)
                        a.activation(kk[p][:, f, 0:ntok[c]], ps_h[f % 2][:, 0:ntok[c]], ACT.Relu).then_inc(s("relu"), 1)
                    both = kk[p][:, 2 * i:2 * i + 2, 0:ntok[c]]
                    act.wait_ge(s("relu"), FB * c + 2 * i + 2)
                    a.activation(both, both, ACT.Square).then_inc(s("kka"), 1)
                return go

            def cr(c):
                act.wait_ge(s("crmm"), c + 1)
                if c >= 2:
                    act.wait_ge(s("p2"), c - 1)
                a.activation(thc[c % 2][:, 0:ntok[c]], ps_cr[:, 0:ntok[c]], ACT.Tanh,
                             scale=0.5).then_inc(s("thc"), 1)

            def outs(c):
                act.wait_ge(s("x3T_mm"), c + 1)
                if c >= 1:
                    act.wait_ge(s("lgmm"), c)
                a.activation(x3T[:, 0:ntok[c]], ps_tb[:, 0:ntok[c]], ACT.Copy).then_inc(s("x3T"), 1)

            def route(c):
                act.wait_ge(s("r1"), c + 1)
                a.activation(ex[:, 0:nt[c], :], lg[:, 0:nt[c], :], ACT.Exp).then_inc(s("rexp"), 1)

            run("act", ln1m=ln1, m3=mscan, s=sscan, vmm=v_copy, rmm=r_tanh, d2=delta, x1m=x1s, kk1=relu_square(0),
                kk2=relu_square(1), cr=cr, x3=outs, r1=route)

            for e in range(E):
                act.wait_ge(w1_in[e], 16)
                a.activation(w1hi_sb[:, e, :], w1raw[e], ACT.Copy).then_inc(s("e_w1hi"), 1)
            a.activation(x3T[:, 0:1], zero[:, 0:1], ACT.Gelu_apprx_tanh)
            def x_hi(e):
                act.wait_ge(s("e_T"), e + 1)
                if e >= 2:
                    act.wait_ge(s("e_h"), FB * (e - 1))
                a.activation(xhi[e % 2], [ps_ta, ps_tb][e % 2][:, :], ACT.Copy).then_inc(s("e_x"), 1)

            x_hi(0)
            x_hi(1)
            for e in range(E):
                p = e % 2
                if e >= 2:
                    act.wait_ge(s("e_y"), e - 1)
                for f in range(FB):
                    act.wait_ge(s("e_h"), FB * e + f + 1)
                    a.activation(kk[p][:, f, :], ps_e[f][:, :], ACT.Gelu_apprx_tanh,
                                 bias=vcol[:, NVEC + e * FB + f:NVEC + e * FB + f + 1]).then_inc(s("e_g"), 1)
                if e + 2 < E:
                    x_hi(e + 2)

        @block.vector
        def _(dve):
            v = nc.vector
            v.memset(zero[:, :], 0.0).then_inc(s("zset"), 1)
            v.memset(ohs[:, 0, :], 0.0).then_inc(s("ohs"), 1)
            def flat(t):
                return t.rearrange("p j c -> p (j c)")

            def stats(k, i, n, src, done):
                for j in range(n):
                    last = v.bn_stats(st[k][i % 2][:, j, :], src(j))
                last.then_inc(done, 1)

            def mean_var(k, i, n, mv, stats_done, done):
                dve.wait_ge(stats_done, i + 1)
                for j in range(n):
                    last = v.bn_aggr(mv[:, j, :], st[k][i % 2][:, j, :])
                last.then_inc(done, 1)

            def vectors():
                dve.wait_ge(s("vt"), 1)
                v.tensor_copy(vcol[:, :], ps_k[:, 0:NVEC + E * FB]).then_inc(s("vcol"), 1)
                dve.wait_ge(s("vcol"), 1)
                v.tensor_scalar(omix[:, :], vcol[:, MK:MK + 5], -1.0, 1.0, ALU.mult, ALU.add).then_inc(s("wmix"), 1)
                v.tensor_scalar(nuh[:, :], vcol[:, U_:U_ + 1], -0.5, None, ALU.mult).then_inc(s("wmix"), 1)
                dve.wait_ge(s("wmix"), 2)
                dve.wait_ge(s("w_in"), 16 * 4)
                for r, m in enumerate((0, 1, 2, 4)):
                    v.tensor_scalar(wm_sb[:, r, 0, :], wt_sb[:, r, :], vcol[:, MK + m:MK + m + 1], None, ALU.mult)\
                        .then_inc(s("wmix"), 1)
                    v.tensor_scalar(wm_sb[:, r, 1, :], wt_sb[:, r, :], omix[:, m:m + 1], None, ALU.mult)\
                        .then_inc(s("wmix"), 1)

            def ln1(c):
                dve.wait_ge(x_in[c], 16)
                stats(0, c, nt[c], lambda j: x_sb[:, t0[c] + j, :], s("ln1_st"))

            def ln1m(c):
                if c >= 2:
                    dve.wait_ge(s("xn"), c - 1)
                mean_var(0, c, nt[c], mv1[c % 2], s("ln1_st"), s("ln1_mv"))
                if c == 0:
                    vectors()

            def carry(c, buf, start, done):
                p = c % 2
                if row0[c]:
                    v.memset(buf[p][:, 0:1], start).then_inc(done, 1)
                    return start
                last = buf[1 - p][:, ntok[c - 1]:ntok[c - 1] + 1]
                v.tensor_copy(buf[p][:, 0:1], last).then_inc(done, 1)
                return last

            def m1(c):
                p, n = c % 2, ntok[c]
                if c >= 1:
                    dve.wait_ge(s("mscan"), c)
                first = carry(c, Mx, NEG_INF, s("m0"))
                dve.wait_ge(s("kmm"), c + 1)
                v.tensor_tensor_scan(Mx[p][:, 1:n + 1], vcol[:, W_:W_ + 1].broadcast_to([P, n]), ps_k[:, 0:n],
                                     first, ALU.add, ALU.max).then_inc(s("mscan"), 1)

            def m2(c):
                p, n = c % 2, ntok[c]
                dve.wait_ge(s("mscan"), c + 1)
                dve.wait_ge(s("m0"), c + 1)
                v.scalar_tensor_tensor(G[p][:, 0:n], Mx[p][:, 0:n], vcol[:, W_:W_ + 1], ps_k[:, 0:n],
                                       ALU.add, ALU.subtract).then_inc(s("gdone"), 1)

            def m3(c):
                p, n = c % 2, ntok[c]
                dve.wait_ge(s("gdone"), c + 1)
                v.tensor_scalar(EF[p][:, 0, 0:n], G[p][:, 0:n], 0.0, None, ALU.min)
                v.tensor_scalar(EF[p][:, 1, 0:n], G[p][:, 0:n], 0.0, None, ALU.max).then_inc(s("efin"), 1)

            def sscan(c):
                p, n = c % 2, ntok[c]
                if c >= 1:
                    dve.wait_ge(s("sscan"), c)
                first = carry(c, Sx, 1.0, s("s0"))
                dve.wait_ge(s("efexp"), c + 1)
                v.tensor_tensor_scan(Sx[p][:, 1:n + 1], EF[p][:, 0, 0:n], EF[p][:, 1, 0:n], first,
                                     ALU.mult, ALU.add).then_inc(s("sscan"), 1)

            def d1(c):
                p, n = c % 2, ntok[c]
                dve.wait_ge(s("lns"), c + 1)
                v.tensor_tensor(LS[p][:, 0:n], LS[p][:, 0:n], G[p][:, 0:n], ALU.add).then_inc(s("delta"), 1)
                if row0[c]:
                    dve.wait_ge(s("delta"), deltas(c) - 1)
                    v.memset(LS[p][:, 0:1], -80.0).then_inc(s("delta"), 1)

            def d2(c):
                p, n = c % 2, ntok[c]
                dve.wait_ge(s("delta"), deltas(c))
                v.tensor_scalar(AB[p][:, 0, 0:n], LS[p][:, 0:n], 0.0, None, ALU.min).then_inc(s("abin"), 1)

            def bv(c):
                p, n = c % 2, ntok[c]
                dve.wait_ge(s("abexp"), c + 1)
                dve.wait_ge(s("v_sb"), c + 1)
                v.scalar_tensor_tensor(AB[p][:, 1, 0:n], AB[p][:, 1, 0:n], 1.0, V[p][:, 0:n], ALU.min, ALU.mult)\
                    .then_inc(s("bv"), 1)

            def aa(c):
                p, n = c % 2, ntok[c]
                if c >= 1:
                    dve.wait_ge(s("ascan"), c)
                first = carry(c, Ax, 0.0, s("a0"))
                dve.wait_ge(s("bv"), c + 1)
                v.tensor_tensor_scan(Ax[p][:, 1:n + 1], AB[p][:, 0, 0:n], AB[p][:, 1, 0:n], first,
                                     ALU.mult, ALU.add).then_inc(s("ascan"), 1)

            def df(c):
                p, n = c % 2, ntok[c]
                dve.wait_ge(s("ascan"), c + 1)
                dve.wait_ge(s("a0"), c + 1)
                if c >= 2:
                    dve.wait_ge(s("ryT"), c - 1)
                v.tensor_tensor(Y[p][:, 0:n], Ax[p][:, 0:n], V[p][:, 0:n], ALU.subtract).then_inc(s("df"), 1)

            def yq(c):
                p, n = c % 2, ntok[c]
                dve.wait_ge(s("th"), c + 1)
                if row0[c]:
                    v.memset(TH[p][:, 0:1], -1.0).then_inc(s("th0"), 1)
                    dve.wait_ge(s("th0"), sum(row0[:c + 1]))
                dve.wait_ge(s("df"), c + 1)
                v.scalar_tensor_tensor(Y[p][:, 0:n], TH[p][:, 0:n], 1.0, Y[p][:, 0:n], ALU.add, ALU.mult)\
                    .then_inc(s("q"), 1)

            def yy(c):
                p, n = c % 2, ntok[c]
                dve.wait_ge(s("q"), c + 1)
                v.scalar_tensor_tensor(Y[p][:, 0:n], Y[p][:, 0:n], 0.5, V[p][:, 0:n], ALU.mult, ALU.add)\
                    .then_inc(s("y"), 1)

            def ry(c):
                p, n = c % 2, ntok[c]
                dve.wait_ge(s("y"), c + 1)
                dve.wait_ge(s("thr"), c + 1)
                v.scalar_tensor_tensor(Y[p][:, 0:n], THR[p][:, 0:n], 1.0, Y[p][:, 0:n], ALU.add, ALU.mult)\
                    .then_inc(s("ry"), 1)

            def x1a(c):
                p, n = c % 2, ntok[c]
                dve.wait_ge(s("ryT"), c + 1)
                if c >= 2:
                    dve.wait_ge(s("xx"), c - 1)
                    dve.wait_ge(s("x2n"), c - 1)
                v.scalar_tensor_tensor(flat(x1[p][:, 0:nt[c], :]), ps_tb[:, 0:n], 0.5,
                                       flat(x_sb[:, t0[c]:t0[c] + nt[c]]), ALU.mult, ALU.add)\
                    .then_inc(s("x1"), 1)

            def x1s(c):
                dve.wait_ge(s("x1"), c + 1)
                stats(1, c, nt[c], lambda j: x1[c % 2][:, j, :], s("ln2_st"))

            def x1m(c):
                if c >= 2:
                    dve.wait_ge(s("x2n"), c - 1)
                mean_var(1, c, nt[c], mv2[c % 2], s("ln2_st"), s("ln2_mv"))

            def ck(c):
                p, n = c % 2, ntok[c]
                dve.wait_ge(s("cx"), c + 1)
                v.scalar_tensor_tensor(cx[p][:, 0:n], h2T[p][:, 1:n + 1], vcol[:, CK:CK + 1], cx[p][:, 0:n],
                                       ALU.mult, ALU.add).then_inc(s("ck"), 1)

            def p2(c):
                p, n = c % 2, ntok[c]
                dve.wait_ge(s("cvmm"), c + 1)
                dve.wait_ge(s("thc"), c + 1)
                v.scalar_tensor_tensor(z[p][:, 0:n], thc[p][:, 0:n], 1.0, ps_cv[:, 0:n],
                                       ALU.add, ALU.mult).then_inc(s("p2"), 1)

            def zz(c):
                p, n = c % 2, ntok[c]
                dve.wait_ge(s("p2"), c + 1)
                dve.wait_ge(s("xx"), c + 1)
                v.scalar_tensor_tensor(z[p][:, 0:n], z[p][:, 0:n], 0.5, flat(x_sb[:, t0[c]:t0[c] + nt[c]]),
                                       ALU.mult, ALU.add).then_inc(s("zz"), 1)

            def zs(c):
                dve.wait_ge(s("zz"), c + 1)
                stats(2, c, nt[c], lambda j: z[c % 2][:, j * C:(j + 1) * C], s("ln3_st"))

            def zm(c):
                mean_var(2, c, nt[c], mv3[:, t0[c]:t0[c] + nt[c]], s("ln3_st"), s("ln3_mv"))

            def x3(c):
                dve.wait_ge(s("rst3"), c + 1)
                for j in range(nt[c]):
                    k = t0[c] + j
                    last = v.tensor_scalar(rows[:, k, 0:C], z[c % 2][:, j * C:(j + 1) * C], mv3[:, k, 0:1],
                                           rs3[:, k:k + 1], ALU.subtract, ALU.mult)
                last.then_inc(s("x3"), 1)

            def wide(t, c):
                return t[:, 0:nt[c]].unsqueeze(2).broadcast_to([P, nt[c], E])

            def logits(c):
                return ps_cr[:, 0:nt[c] * E].rearrange("p (j e) -> p j e", e=E)

            def ranks(c):
                return ps_cr[:, nt[c] * E:2 * nt[c] * E].rearrange("p (j e) -> p j e", e=E)

            def r0(c):
                dve.wait_ge(s("lgmm"), c + 1)
                v.tensor_reduce(mx[:, 0:nt[c]], logits(c), AX.X, ALU.max).then_inc(s("r0"), 1)

            def r1(c):
                dve.wait_ge(s("r0"), c + 1)
                v.tensor_tensor(lg[:, 0:nt[c], :], logits(c), wide(mx, c), ALU.subtract).then_inc(s("r1"), 1)

            def rc(c):
                dve.wait_ge(s("r1"), c + 1)
                v.scalar_tensor_tensor(cand[:, 0:nt[c], :], lg[:, 0:nt[c], :], 0.0, iota_m[:, 0:nt[c], :], ALU.is_equal, ALU.mult)\
                    .then_inc(s("rcand"), 1)

            def ri(c):
                dve.wait_ge(s("rcand"), c + 1)
                v.tensor_reduce(eidx[:, 0:nt[c]], cand[:, 0:nt[c], :], AX.X, ALU.min).then_inc(s("ridx"), 1)

            def ohot(c):
                dve.wait_ge(s("ridx"), c + 1)
                v.tensor_tensor(oh[:, 0:nt[c], :], iota_m[:, 0:nt[c], :], wide(eidx, c), ALU.is_equal).then_inc(s("oh"), 1)

            def r2(c):
                dve.wait_ge(s("rexp"), c + 1)
                v.tensor_reduce(sm[:, 0:nt[c]], ex[:, 0:nt[c], :], AX.X, ALU.add).then_inc(s("rsum"), 1)
                dve.wait_ge(s("rankmm"), c + 1)
                v.tensor_tensor(loc8[:, 0:nt[c], :], ranks(c), oh[:, 0:nt[c], :], ALU.mult).then_inc(s("rloc8"), 1)
                v.tensor_reduce(ohr[:, :], oh[:, 0:nt[c], :].rearrange("p j e -> p e j"), AX.X, ALU.add)\
                    .then_inc(s("rsub"), 1)
                dve.wait_ge(s("rsum"), c + 1)
                v.reciprocal(rows[:, t0[c]:t0[c] + nt[c], GATE], sm[:, 0:nt[c]]).then_inc(s("rgate"), 1)
                dve.wait_ge(s("rloc8"), c + 1)
                v.tensor_reduce(loc[:, 0:nt[c]], loc8[:, 0:nt[c], :], AX.X, ALU.add).then_inc(s("rloc"), 1)

            def r3(c):
                p = c % 2
                dve.wait_ge(s("rsub"), c + 1)
                v.tensor_tensor(ohs[:, 1 - p, :], ohs[:, p, :], ohr[:, :], ALU.add).then_inc(s("ohs"), 1)
                dve.wait_ge(s("rloc"), c + 1)
                v.scalar_tensor_tensor(slot[:, 0:nt[c]], eidx[:, 0:nt[c]], float(CAP), loc[:, 0:nt[c]], ALU.mult, ALU.add)
                v.tensor_scalar(pen[:, 0:nt[c]], loc[:, 0:nt[c]], float(CAP), float(4 * N), ALU.is_ge, ALU.mult)\
                    .then_inc(s("rslot"), 1)

            def r4(c):
                dve.wait_ge(s("rslot"), c + 1)
                if c >= 2:
                    dve.wait_ge(scat[c - 2], 16 * nt[c - 2])
                v.scalar_tensor_tensor(sidx[c % 2][:, 0:nt[c]], slot[:, 0:nt[c]], float(E * CAP), pen[:, 0:nt[c]], ALU.add, ALU.add)\
                    .then_inc(s("sidx"), 1)

            run("dve", ln1=ln1, ln1m=ln1m, m1=m1, m2=m2, m3=m3, s=sscan, d1=d1, d2=d2, bv=bv, aa=aa, df=df, yq=yq, yy=yy,
                ry=ry, x1=x1a, x1s=x1s, x1m=x1m, ck=ck, p2=p2, zz=zz, zs=zs, zm=zm,
                x3=x3, r0=r0, r1=r1, rc=rc, ri=ri, oh=ohot, r2=r2, r3=r3, r4=r4)

            for e in range(E):
                dve.wait_ge(s("e_w1hi"), e + 1)
                v.tensor_tensor(w1lo_sb[:, e, :], w1raw[e], w1hi_sb[:, e, :].bitcast(F32), ALU.subtract)\
                    .then_inc(s("e_w1lo"), 1)

            def rest(e):
                p = e % 2
                dve.wait_ge(s("e_x"), e + 1)
                v.tensor_tensor(xlo[p], [ps_ta, ps_tb][p][:, :], xhi[p].bitcast(F32), ALU.subtract)\
                    .then_inc(s("e_xlo"), 1)
                v.tensor_copy(tid[:, e, :], er[:, e, :, TOK]).then_inc(s("e_tid"), 1)

            def gated(u):
                e, j0, n = UNITS[u]
                p = u % 2
                zt = [z[p][:, j * C:(j + 1) * C] for j in range(n)]
                dve.wait_ge(s("e_y"), u + 1)
                if u >= 2:
                    dve.wait_ge(s("e_norm"), u - 1)
                yb = [ps_cv, ps_cr][p][:, 0:n * C].rearrange("p (j c) -> p j c", c=C)
                v.tensor_tensor(z[p][:, 0:n * C].rearrange("p (j c) -> p j c", c=C), yb,
                                b2_sb[e].unsqueeze(1).broadcast_to([P, n, C]), ALU.add).then_inc(s("e_yb"), 1)
                dve.wait_ge(s("e_yb"), u + 1)
                for j in range(n):
                    last = v.scalar_tensor_tensor(zt[j], zt[j], er[:, e, j0 + j, GATE:GATE + 1],
                                                  er[:, e, j0 + j, 0:C], ALU.mult, ALU.add)
                last.then_inc(s("e_z"), 1)
                dve.wait_ge(s("e_z"), u + 1)
                stats(0, u, n, lambda j: zt[j], s("e_st"))
                mean_var(0, u, n, mv1[p], s("e_st"), s("e_mv"))

            def finish(u):
                p = u % 2
                dve.wait_ge(s("e_rst"), u + 1)
                if u >= NEO:
                    dve.wait_ge(osc[u % NEO], 16 * sent(u))
                for j in range(UNITS[u][2]):
                    last = v.tensor_scalar(eo[u % NEO][:, j, :], z[p][:, j * C:(j + 1) * C], mv1[p][:, j, 0:1],
                                           rs[:, 0, p, j:j + 1], ALU.subtract, ALU.mult)
                last.then_inc(s("e_norm"), 1)

            rest(0)
            rest(1)

            dve.wait_ge(s("dsc"), 1)
            for c in range(NCH):
                dve.wait_ge(scat[c], 16 * nt[c])
                for k in range(t0[c], t0[c] + nt[c]):
                    last = v.tensor_scalar(rows[:, k, 0:C], rows[:, k, 0:C], dsc[:, 2, k:k + 1], None, ALU.mult)
                last.then_inc(s("drop"), 1)

            dve.wait_ge(s("b2_in"), 16 * E)
            for u in range(NU - 2):
                if u + 2 < E:
                    rest(u + 2)
                gated(u)
                finish(u)
            gated(NU - 2)
            gated(NU - 1)
            finish(NU - 2)
            finish(NU - 1)

        @block.tensor
        def _(pe):
            t_ = nc.tensor
            NV = NVEC + E * FB
            pe.wait_ge(s("cst"), 6)
            for _ in range(16):
                t_.matmul(ps_h[0][:, 0:P], ident[:, :], ident[:, :], start=True, stop=True)
            pe.wait_ge(s("v_in"), 16 * 12)
            t_.transpose(ps_k[:, 0:NV], vrows[:, :], ident[0:NV, 0:NV]).then_inc(s("vt"), 1)

            def turn(n, dst, src, done):
                for j in range(n):
                    last = t_.transpose(dst[:, j * TILE:(j + 1) * TILE], src(j), ident[:, :])
                last.then_inc(done, 1)

            def mixed(dst, r, c, done):
                t_.matmul(dst[:, 0:ntok[c]], wm_sb[:, r, 0, :], hT[c % 2][:, 1:ntok[c] + 1], start=True, stop=False)
                t_.matmul(dst[:, 0:ntok[c]], wm_sb[:, r, 1, :], hT[c % 2][:, 0:ntok[c]], start=False, stop=True)\
                    .then_inc(done, 1)

            ta_users = (("ln1m", s("hT")), ("x1m", s("h2T")))
            tb_users = (("ry", s("x1")), ("x3", s("x3T")))

            def ln1(c):
                pe.wait_ge(s("xn"), c + 1)
                freed(pe, "ln1m", c, *ta_users)
                turn(nt[c], ps_ta, lambda j: xn[c % 2][:, j, :], s("xnT"))

            def kmm(c):
                if c == 0:
                    pe.wait_ge(s("wmix"), 4)
                pe.wait_ge(s("hT"), c + 1)
                pe.wait_ge(s("h0"), c + 1)
                if c >= 1:
                    pe.wait_ge(s("gdone"), c)
                mixed(ps_k, 0, c, s("kmm"))

            def vmm(c):
                if c == 0:
                    pe.wait_ge(s("wmix"), 10)
                if c >= 1:
                    pe.wait_ge(s("thr"), c)
                mixed(ps_vr, 1, c, s("vmm"))

            def rmm(c):
                pe.wait_ge(s("v_sb"), c + 1)
                mixed(ps_vr, 2, c, s("rmm"))

            def y2(c):
                pe.wait_ge(s("ry"), c + 1)
                freed(pe, "ry", c, *tb_users)
                turn(nt[c], ps_tb, lambda j: Y[c % 2][:, j * TILE:(j + 1) * TILE], s("ryT"))

            def x1s(c):
                pe.wait_ge(s("x2n"), c + 1)
                freed(pe, "x1m", c, *ta_users)
                turn(nt[c], ps_ta, lambda j: x2n[c % 2][:, j, :], s("x2nT"))

            def hidden(i):
                def go(c):
                    if c == 0:
                        pe.wait_ge(s("wc_in"), 16 * 3)
                    pe.wait_ge(s("ck"), c + 1)
                    for f in (2 * i, 2 * i + 1):
                        n = FB * c + f
                        if n >= 2:
                            pe.wait_ge(s("relu"), n - 1)
                        t_.matmul(ps_h[f % 2][:, 0:ntok[c]], wck_sb[:, f * P:(f + 1) * P], cx[c % 2][:, 0:ntok[c]], start=True,
                                  stop=True).then_inc(s("hmm"), 1)
                return go

            def cr(c):
                pe.wait_ge(s("h2T"), c + 1)
                pe.wait_ge(s("h20"), c + 1)
                if c == 0:
                    pe.wait_ge(s("wmix"), 10)
                freed(pe, "cr", c, ("lg", s("rloc8")))
                for j in range(nt[c]):
                    o = ps_cr[:, j * C:(j + 1) * C]
                    h2 = h2T[c % 2]
                    t_.matmul(o, h2[:, 1 + j * TILE:1 + (j + 1) * TILE], wm_sb[:, 3, 0, :], start=True, stop=False)
                    last = t_.matmul(o, h2[:, j * TILE:(j + 1) * TILE], wm_sb[:, 3, 1, :], start=False, stop=True)
                last.then_inc(s("crmm"), 1)

            def cv(c):
                p = c % 2
                pe.wait_ge(s("kka"), FB // 2 * (c + 1))
                if c >= 1:
                    pe.wait_ge(s("p2"), c)
                for j in range(nt[c]):
                    for f in range(FB):
                        last = t_.matmul(ps_cv[:, j * C:(j + 1) * C], kk[p][:, f, j * TILE:(j + 1) * TILE],
                                         wcv_sb[:, f, :], start=(f == 0), stop=(f == FB - 1))
                last.then_inc(s("cvmm"), 1)

            def n3(c):
                pe.wait_ge(s("x3"), c + 1)
                freed(pe, "x3", c, *tb_users)
                turn(nt[c], ps_tb, lambda j: rows[:, t0[c] + j, 0:C], s("x3T_mm"))

            def lgmm(c):
                pe.wait_ge(s("x3T"), c + 1)
                freed(pe, "lg", c, ("cr", s("thc")), ("lg", s("rloc8")))
                for j in range(nt[c]):
                    last = t_.matmul(ps_cr[:, j * E:(j + 1) * E], x3T[:, j * TILE:(j + 1) * TILE], wg_sb[:, :],
                                     start=True, stop=True)
                last.then_inc(s("lgmm"), 1)

            def r1(c):
                n = nt[c]
                R = n * E
                pe.wait_ge(s("oh"), c + 1)
                pe.wait_ge(s("ohs"), c + 1)
                ohf = oh[:, 0:n, :].rearrange("p j e -> p (j e)")
                t_.matmul(ps_cr[:, R:2 * R], tri[:, :], ohf, start=True, stop=False)
                t_.matmul(ps_cr[:, R:2 * R].rearrange("p (j e) -> p j e", e=E), ones[:, :],
                          ohs[:, c % 2:c % 2 + 1, :].broadcast_to([P, n, E]), start=False, stop=False)
                for i in range(n - 1):
                    last = t_.matmul(ps_cr[:, R + (i + 1) * E:2 * R].rearrange("p (j e) -> p j e", e=E), ones[:, :],
                                     oh[:, i:i + 1, :].broadcast_to([P, n - 1 - i, E]),
                                     start=False, stop=(i == n - 2))
                last.then_inc(s("rankmm"), 1)

            run("pe", ln1m=ln1, kmm=kmm, vmm=vmm, rmm=rmm, ry=y2, x1m=x1s, ck=hidden(0), kk1=hidden(1), cr=cr, cv=cv,
                x3=n3, lg=lgmm, oh=r1)

            pe.wait_ge(s("relu"), FB * NCH)
            for _ in range(8):
                t_.matmul(ps_h[0][:, :], ident[:, :], wck_sb[:, :], start=True, stop=True)

            pe.wait_ge(s("we_in"), 16 * E)

            def second(e):
                p = e % 2
                pe.wait_ge(s("e_g"), FB * (e + 1))
                for u, (_, j0, n) in ((u, t) for u, t in enumerate(UNITS) if t[0] == e):
                    if u >= 2:
                        pe.wait_ge(s("e_yb"), u - 1)
                    if u == 1:
                        pe.wait_ge(s("rloc8"), NCH)
                    for j in range(n):
                        for f in range(FB):
                            t = slice((j0 + j) * TILE, (j0 + j + 1) * TILE)
                            last = t_.matmul([ps_cv, ps_cr][u % 2][:, j * C:(j + 1) * C], kk[p][:, f, t],
                                             w2_sb[:, e, f, :], start=(f == 0), stop=(f == FB - 1))
                    last.then_inc(s("e_y"), 1)

            def expand(e):
                p = e % 2
                pe.wait_ge(e_in[e], 16)
                if e >= 2:
                    pe.wait_ge(s("e_xlo"), e - 1)
                turn(SPE, [ps_ta, ps_tb][p], lambda j: er[:, e, j, 0:C], s("e_T"))

            expand(0)
            expand(1)
            for e in range(E):
                p = e % 2
                pe.wait_ge(s("e_w1lo"), e + 1)
                pe.wait_ge(s("e_x"), e + 1)
                pe.wait_ge(s("e_xlo"), e + 1)
                for f in range(FB):
                    n = FB * e + f
                    if n >= 4:
                        pe.wait_ge(s("e_g"), n - 3)
                    cols = slice(f * P, (f + 1) * P)
                    t_.matmul(ps_e[f][:, :], w1hi_sb[:, e, cols], xhi[p], start=True, stop=False)
                    t_.matmul(ps_e[f][:, :], w1hi_sb[:, e, cols], xlo[p], start=False, stop=False)
                    t_.matmul(ps_e[f][:, :], w1lo_sb[:, e, cols], xhi[p], start=False, stop=True).then_inc(s("e_h"), 1)
                if e + 2 < E:
                    expand(e + 2)
                if 1 <= e:
                    second(e - 1)
            second(E - 1)


_INS = ['L0_attn_x', 'L0_attn_time_decay', 'L0_attn_time_first', 'L0_attn_w_tk', 'L0_attn_w_tv', 'L0_attn_w_tr',
        'L0_attn_w_ck', 'L0_attn_w_cv', 'L0_attn_w_cr', 'L0_attn_ln1_g', 'L0_attn_ln1_b', 'L0_attn_ln2_g',
        'L0_attn_ln2_b', 'L0_attn_mix_k', 'L0_attn_mix_v', 'L0_attn_mix_r', 'L0_attn_cmix_k', 'L0_attn_cmix_r',
        'L0_ffn_wg', 'L0_ffn_w1', 'L0_ffn_b1', 'L0_ffn_w2', 'L0_ffn_b2']
_OUTS = [((2, 2048, 128), 'float32')]


def kernel(**inputs):
    import numpy as _np
    import concourse.bacc as _bacc
    from concourse import mybir as _mybir
    from concourse.bass_utils import run_bass_kernel_spmd as _run

    nc = _bacc.Bacc("TRN2", target_bir_lowering=False, num_devices=1)
    arrays, args = {}, []
    for name in _INS:
        a = _np.ascontiguousarray(inputs[name])
        arrays[f"in_{name}_dram"] = a
        args.append(nc.dram_tensor(f"in_{name}_dram", a.shape, _mybir.dt.from_np(a.dtype), kind="ExternalInput").ap())
    for i, (shape, dtype) in enumerate(_OUTS):
        dt = _mybir.dt.from_np(_np.dtype(dtype))
        args.append(nc.dram_tensor(f"out_{i}_dram", shape, dt, kind="ExternalOutput").ap())
    rwkv_moe_kernel(nc, *args)
    r = _run(nc, [arrays], core_ids=[0])
    return r.results[0]["out_0_dram"]
```
